# Optimizing a Trainium2 kernel written in Bass

```python
import numpy as np
import jax
import jax.numpy as jnp

def _softmax(x, axis=-1):
    return jax.nn.softmax(x, axis=axis)

def _gelu(x):
    return jax.nn.gelu(x, approximate=True)

def _silu(x):
    return jax.nn.silu(x)

def _sigmoid(x):
    return jax.nn.sigmoid(x)

def _layernorm(x, axis=-1, eps=1e-05):
    m = jnp.mean(x, axis=axis, keepdims=True)
    v = jnp.var(x, axis=axis, keepdims=True)
    return (x - m) / jnp.sqrt(v + eps)

def _scatter_add(tgt, idx, src, axis=0):
    return tgt.at[idx].add(src)

def _segment_sum(src, seg, n):
    return jax.ops.segment_sum(src, seg, n)
kernel_name = 'mk_perceiver_d1_seqx_r8_eca460'

def setup_inputs(seed: int=0):
    np.random.seed(seed)
    _w = jnp.asarray

    def _rec_inputs():
        import jax
        import jax.numpy as jnp
        _rk = jax.random.key(seed)
        x = -0.0003929 + 0.9999 * jax.random.normal(jax.random.fold_in(_rk, 1), (32, 64, 256), jnp.float32)
        _lenS = 64 - jax.random.randint(jax.random.fold_in(_rk, 7), (32,), 0, max(1, 64 // 4) + 1, jnp.int32)
        _lenS2 = 1601 - jax.random.randint(jax.random.fold_in(_rk, 8), (32,), 0, max(1, 1601 // 4) + 1, jnp.int32)
        _ctx_2048P = jax.random.normal(jax.random.fold_in(_rk, 11), (32, 16, 256), jnp.float32)
        _ctx_2048c = jax.random.dirichlet(jax.random.fold_in(_rk, 511), 0.3 * jnp.ones((16,), jnp.float32), (32, 1601))
        _ctx_2048t = jnp.einsum('bsk,bkd->bsd', _ctx_2048c, _ctx_2048P)
        _ctx_2048t = _ctx_2048t * jax.lax.rsqrt(jnp.mean(jnp.square(_ctx_2048t)) + 1e-12) * 0.953939
        ctx_2048 = 4.13588e-05 + 0.999923 * (_ctx_2048t + 0.3 * jax.random.normal(jax.random.fold_in(_rk, 611), (32, 1601, 256), jnp.float32))
        return (x, ctx_2048)
    x, ctx_2048 = _rec_inputs()

    def _L0_xattn_setup():
        import jax, jax.numpy as jnp
        import numpy as np
        HIDDEN = 256
        N_HEADS = 16
        N_KV_HEADS = 4
        HEAD_DIM = 128
        EPS = 1e-06

        def rms_norm(x, w, eps=EPS):
            xf = x.astype(jnp.float32)
            var = jnp.mean(xf * xf, axis=-1, keepdims=True)
            return w * (xf * jax.lax.rsqrt(var + eps)).astype(x.dtype)
        key = jax.random.key(seed)
        ks = jax.random.split(key, 8)
        B, S, S_ENC = (4, 256, 128)
        inner = N_HEADS * HEAD_DIM
        kv_dim = N_KV_HEADS * HEAD_DIM
        s = 0.02
        return {'hidden_states': jax.random.normal(ks[0], (B, S, HIDDEN), jnp.float32), 'encoder_hidden_states': jax.random.normal(ks[1], (B, S_ENC, HIDDEN), jnp.float32), 'Wq': jax.random.normal(ks[2], (HIDDEN, inner), jnp.float32) * s, 'Wk': jax.random.normal(ks[3], (HIDDEN, kv_dim), jnp.float32) * s, 'Wv': jax.random.normal(ks[4], (HIDDEN, kv_dim), jnp.float32) * s, 'Wo': jax.random.normal(ks[5], (inner, HIDDEN), jnp.float32) * s, 'q_norm_w': jnp.ones((HEAD_DIM,), jnp.float32), 'k_norm_w': jnp.ones((HEAD_DIM,), jnp.float32)}
    _L0_xattn_all = _L0_xattn_setup()
    _L0_xattn_in = {k: v for k, v in _L0_xattn_all.items() if k in ('Wq', 'Wk', 'Wv', 'Wo', 'q_norm_w', 'k_norm_w')}
    del _L0_xattn_all

    def _L0_attn_setup():
        import jax, jax.numpy as jnp
        import numpy as np
        B, S, H, R, L = (4, 256, 256, 256, 256)
        W_SCALE = 0.02

        def _reference_tuple_inner(x, w_f, w_i, w_v, w_q, w_ro, w_aux, w_up, w_gate, w_down, init_state):
            b, s, _ = x.shape
            f = jnp.tanh(jnp.einsum('bsh,hr->bsr', x, w_f))
            g = jax.nn.sigmoid(jnp.einsum('bsh,hr->bsr', x, w_i)) * jax.nn.silu(jnp.einsum('bsh,hr->bsr', x, w_v))

            def step(state, fg):
                ft, gt = fg
                state = ft * state + gt
                return (state, state)
            s0 = jnp.broadcast_to(init_state, (b, init_state.shape[0]))
            _, states = jax.lax.scan(step, s0, (jnp.swapaxes(f, 0, 1), jnp.swapaxes(g, 0, 1)))
            states = jnp.swapaxes(states, 0, 1)
            q = jnp.einsum('bsh,hr->bsr', x, w_q)
            readout = jax.nn.silu(q * states)
            local = jnp.einsum('bsl,lh->bsh', jnp.einsum('bsh,hl->bsl', x, w_up) * jax.nn.silu(jnp.einsum('bsh,hl->bsl', x, w_gate)), w_down)
            out = jnp.einsum('bsr,rh->bsh', readout, w_ro) + local
            aux_pred = jnp.einsum('bsr,rh->bsh', jax.nn.silu(states[:, :-1]), w_aux)
            aux_target = jax.lax.stop_gradient(x[:, 1:])
            aux_loss = jnp.mean((aux_pred - aux_target) ** 2)
            return (out, aux_loss)
        key = jax.random.key(seed)
        ks = jax.random.split(key, 11)
        w = lambda k, shp: jax.random.normal(k, shp, jnp.float32) * W_SCALE
        return {'x': jax.random.normal(ks[0], (B, S, H), jnp.float32), 'w_f': w(ks[1], (H, R)), 'w_i': w(ks[2], (H, R)), 'w_v': w(ks[3], (H, R)), 'w_q': w(ks[4], (H, R)), 'w_ro': w(ks[5], (R, H)), 'w_aux': w(ks[6], (R, H)), 'w_up': w(ks[7], (H, L)), 'w_gate': w(ks[8], (H, L)), 'w_down': w(ks[9], (L, H)), 'init_state': jnp.zeros((R,), jnp.float32)}
    _L0_attn_all = _L0_attn_setup()
    _L0_attn_in = {k: v for k, v in _L0_attn_all.items() if k in ('w_f', 'w_i', 'w_v', 'w_q', 'w_ro', 'w_aux', 'w_up', 'w_gate', 'w_down', 'init_state')}
    del _L0_attn_all

    def _L0_ffn_setup():
        import jax, jax.numpy as jnp
        import numpy as np
        B, S, D = (2, 256, 256)
        F = 128
        E = 64
        K = 8
        C = 128
        NORM_TOPK = False

        def _moe(x, gate_w, w_gate, w_up, w_down):
            b, s, d = x.shape
            T = b * s
            x2 = x.reshape(T, d)
            logits = x2 @ gate_w.T
            probs = jax.nn.softmax(logits.astype(jnp.float32), axis=-1)
            top_w, top_i = jax.lax.top_k(probs, K)
            if NORM_TOPK:
                top_w = top_w / jnp.sum(top_w, axis=-1, keepdims=True)
            top_w = top_w.astype(x.dtype)
            flat_e = top_i.reshape(-1)
            flat_w = top_w.reshape(-1)
            tok = jnp.arange(T * K) // K
            onehot = jax.nn.one_hot(flat_e, E, dtype=jnp.int32)
            pos = jnp.sum(jnp.cumsum(onehot, axis=0) * onehot, axis=-1) - 1
            valid = pos < C
            loc = flat_e * C + jnp.minimum(pos, C - 1)
            flat_w = jnp.where(valid, flat_w, 0.0)
            safe_loc = jnp.where(valid, loc, E * C)
            xg = jnp.zeros((E * C + 1, d), dtype=x.dtype).at[safe_loc].set(x2[tok])[:E * C]
            xg = xg.reshape(E, C, d)
            h = jax.nn.silu(jnp.einsum('ecd,edf->ecf', xg, w_gate)) * jnp.einsum('ecd,edf->ecf', xg, w_up)
            y = jnp.einsum('ecf,efd->ecd', h, w_down).reshape(E * C, d)
            y_tok = y[loc] * flat_w[:, None]
            out = jnp.zeros((T, d), dtype=x.dtype).at[tok].add(y_tok)
            return out.reshape(b, s, d)
        key = jax.random.key(seed)
        ks = jax.random.split(key, 5)
        scale = 0.02
        return {'hidden_states': jax.random.normal(ks[0], (B, S, D), dtype=jnp.float32), 'gate_w': jax.random.normal(ks[1], (E, D), dtype=jnp.float32) * scale, 'w_gate': jax.random.normal(ks[2], (E, D, F), dtype=jnp.float32) * scale, 'w_up': jax.random.normal(ks[3], (E, D, F), dtype=jnp.float32) * scale, 'w_down': jax.random.normal(ks[4], (E, F, D), dtype=jnp.float32) * scale}
    _L0_ffn_all = _L0_ffn_setup()
    _L0_ffn_in = {k: v for k, v in _L0_ffn_all.items() if k in ('gate_w', 'w_gate', 'w_up', 'w_down')}
    del _L0_ffn_all
    return {'x': x, 'ctx_2048': ctx_2048, 'L0_xattn_Wq': _L0_xattn_in['Wq'], 'L0_xattn_Wk': _L0_xattn_in['Wk'], 'L0_xattn_Wv': _L0_xattn_in['Wv'], 'L0_xattn_Wo': _L0_xattn_in['Wo'], 'L0_xattn_q_norm_w': _L0_xattn_in['q_norm_w'], 'L0_xattn_k_norm_w': _L0_xattn_in['k_norm_w'], 'L0_attn_w_f': _L0_attn_in['w_f'], 'L0_attn_w_i': _L0_attn_in['w_i'], 'L0_attn_w_v': _L0_attn_in['w_v'], 'L0_attn_w_q': _L0_attn_in['w_q'], 'L0_attn_w_ro': _L0_attn_in['w_ro'], 'L0_attn_w_aux': _L0_attn_in['w_aux'], 'L0_attn_w_up': _L0_attn_in['w_up'], 'L0_attn_w_gate': _L0_attn_in['w_gate'], 'L0_attn_w_down': _L0_attn_in['w_down'], 'L0_attn_init_state': _L0_attn_in['init_state'], 'L0_ffn_gate_w': _L0_ffn_in['gate_w'], 'L0_ffn_w_gate': _L0_ffn_in['w_gate'], 'L0_ffn_w_up': _L0_ffn_in['w_up'], 'L0_ffn_w_down': _L0_ffn_in['w_down']}

def reference(x, ctx_2048, L0_xattn_Wq, L0_xattn_Wk, L0_xattn_Wv, L0_xattn_Wo, L0_xattn_q_norm_w, L0_xattn_k_norm_w, L0_attn_w_f, L0_attn_w_i, L0_attn_w_v, L0_attn_w_q, L0_attn_w_ro, L0_attn_w_aux, L0_attn_w_up, L0_attn_w_gate, L0_attn_w_down, L0_attn_init_state, L0_ffn_gate_w, L0_ffn_w_gate, L0_ffn_w_up, L0_ffn_w_down):
    import jax
    import jax.numpy as jnp

    def _L0_xattn_ref(hidden_states, encoder_hidden_states, Wq, Wk, Wv, Wo, q_norm_w, k_norm_w):
        import jax, jax.numpy as jnp
        import numpy as np
        HIDDEN = 256
        N_HEADS = 16
        N_KV_HEADS = 4
        HEAD_DIM = 128
        EPS = 1e-06

        def rms_norm(x, w, eps=EPS):
            xf = x.astype(jnp.float32)
            var = jnp.mean(xf * xf, axis=-1, keepdims=True)
            return w * (xf * jax.lax.rsqrt(var + eps)).astype(x.dtype)
        B, S, _ = hidden_states.shape
        S_enc = encoder_hidden_states.shape[1]
        groups = N_HEADS // N_KV_HEADS
        scale = 1.0 / HEAD_DIM ** 0.5
        q = (hidden_states @ Wq).reshape(B, S, N_HEADS, HEAD_DIM)
        k = (encoder_hidden_states @ Wk).reshape(B, S_enc, N_KV_HEADS, HEAD_DIM)
        v = (encoder_hidden_states @ Wv).reshape(B, S_enc, N_KV_HEADS, HEAD_DIM)
        q = rms_norm(q, q_norm_w)
        k = rms_norm(k, k_norm_w)
        k = jnp.repeat(k, groups, axis=2)
        v = jnp.repeat(v, groups, axis=2)
        scores = jnp.einsum('bqhd,bkhd->bhqk', q, k) * scale
        probs = jax.nn.softmax(scores, axis=-1)
        out = jnp.einsum('bhqk,bkhd->bqhd', probs, v)
        out = out.reshape(B, S, N_HEADS * HEAD_DIM)
        return out @ Wo

    def _L0_attn_ref(x, w_f, w_i, w_v, w_q, w_ro, w_aux, w_up, w_gate, w_down, init_state):
        import jax, jax.numpy as jnp
        import numpy as np
        B, S, H, R, L = (4, 256, 256, 256, 256)
        W_SCALE = 0.02

        def _reference_tuple_inner(x, w_f, w_i, w_v, w_q, w_ro, w_aux, w_up, w_gate, w_down, init_state):
            b, s, _ = x.shape
            f = jnp.tanh(jnp.einsum('bsh,hr->bsr', x, w_f))
            g = jax.nn.sigmoid(jnp.einsum('bsh,hr->bsr', x, w_i)) * jax.nn.silu(jnp.einsum('bsh,hr->bsr', x, w_v))

            def step(state, fg):
                ft, gt = fg
                state = ft * state + gt
                return (state, state)
            s0 = jnp.broadcast_to(init_state, (b, init_state.shape[0]))
            _, states = jax.lax.scan(step, s0, (jnp.swapaxes(f, 0, 1), jnp.swapaxes(g, 0, 1)))
            states = jnp.swapaxes(states, 0, 1)
            q = jnp.einsum('bsh,hr->bsr', x, w_q)
            readout = jax.nn.silu(q * states)
            local = jnp.einsum('bsl,lh->bsh', jnp.einsum('bsh,hl->bsl', x, w_up) * jax.nn.silu(jnp.einsum('bsh,hl->bsl', x, w_gate)), w_down)
            out = jnp.einsum('bsr,rh->bsh', readout, w_ro) + local
            aux_pred = jnp.einsum('bsr,rh->bsh', jax.nn.silu(states[:, :-1]), w_aux)
            aux_target = jax.lax.stop_gradient(x[:, 1:])
            aux_loss = jnp.mean((aux_pred - aux_target) ** 2)
            return (out, aux_loss)
        return _reference_tuple_inner(x, w_f, w_i, w_v, w_q, w_ro, w_aux, w_up, w_gate, w_down, init_state)[0]

    def _L0_ffn_ref(hidden_states, gate_w, w_gate, w_up, w_down):
        import jax, jax.numpy as jnp
        import numpy as np
        B, S, D = (2, 256, 256)
        F = 128
        E = 64
        K = 8
        C = 128
        NORM_TOPK = False

        def _moe(x, gate_w, w_gate, w_up, w_down):
            b, s, d = x.shape
            T = b * s
            x2 = x.reshape(T, d)
            logits = x2 @ gate_w.T
            probs = jax.nn.softmax(logits.astype(jnp.float32), axis=-1)
            top_w, top_i = jax.lax.top_k(probs, K)
            if NORM_TOPK:
                top_w = top_w / jnp.sum(top_w, axis=-1, keepdims=True)
            top_w = top_w.astype(x.dtype)
            flat_e = top_i.reshape(-1)
            flat_w = top_w.reshape(-1)
            tok = jnp.arange(T * K) // K
            onehot = jax.nn.one_hot(flat_e, E, dtype=jnp.int32)
            pos = jnp.sum(jnp.cumsum(onehot, axis=0) * onehot, axis=-1) - 1
            valid = pos < C
            loc = flat_e * C + jnp.minimum(pos, C - 1)
            flat_w = jnp.where(valid, flat_w, 0.0)
            safe_loc = jnp.where(valid, loc, E * C)
            xg = jnp.zeros((E * C + 1, d), dtype=x.dtype).at[safe_loc].set(x2[tok])[:E * C]
            xg = xg.reshape(E, C, d)
            h = jax.nn.silu(jnp.einsum('ecd,edf->ecf', xg, w_gate)) * jnp.einsum('ecd,edf->ecf', xg, w_up)
            y = jnp.einsum('ecf,efd->ecd', h, w_down).reshape(E * C, d)
            y_tok = y[loc] * flat_w[:, None]
            out = jnp.zeros((T, d), dtype=x.dtype).at[tok].add(y_tok)
            return out.reshape(b, s, d)
        return _moe(hidden_states, gate_w, w_gate, w_up, w_down)
    x = x + _L0_xattn_ref(_layernorm(x, axis=-1), ctx_2048, L0_xattn_Wq, L0_xattn_Wk, L0_xattn_Wv, L0_xattn_Wo, L0_xattn_q_norm_w, L0_xattn_k_norm_w)
    x = x + _L0_attn_ref(_layernorm(x, axis=-1), L0_attn_w_f, L0_attn_w_i, L0_attn_w_v, L0_attn_w_q, L0_attn_w_ro, L0_attn_w_aux, L0_attn_w_up, L0_attn_w_gate, L0_attn_w_down, L0_attn_init_state)
    x = x + _L0_ffn_ref(_layernorm(x, axis=-1), L0_ffn_gate_w, L0_ffn_w_gate, L0_ffn_w_up, L0_ffn_w_down)
    return x

_drawn_inputs = setup_inputs


def setup_inputs(seed=0):
    import zlib

    import numpy as np

    out = dict(_drawn_inputs(seed))
    spreads = {'L0_xattn_q_norm_w': (1.0, 0.6),
     'L0_xattn_k_norm_w': (1.0, 0.6),
     'L0_attn_init_state': (0.0, 0.8)}
    factors = {'L0_attn_w_f': 8.0,
     'L0_attn_w_i': 8.0,
     'L0_attn_w_v': 8.0,
     'L0_attn_w_q': 8.0,
     'L0_attn_w_ro': 8.0,
     'L0_attn_w_up': 3.41,
     'L0_attn_w_gate': 3.451,
     'L0_attn_w_down': 3.399,
     'L0_ffn_gate_w': 8.0,
     'L0_ffn_w_gate': 8.0,
     'L0_ffn_w_up': 8.0,
     'L0_ffn_w_down': 8.0}
    for name, (base, spread) in spreads.items():
        noise = np.random.default_rng([zlib.crc32(name.encode()), seed]).standard_normal(out[name].shape)
        drawn = base * np.exp(spread * noise) if base else spread * noise
        out[name] = jnp.asarray(drawn.astype(out[name].dtype))
    for name, factor in factors.items():
        out[name] = (out[name] * factor).astype(out[name].dtype)
    return out
```

```python
from contextlib import ExitStack

import concourse.bass as bass
from concourse import mybir

F32 = mybir.dt.float32
F32R = mybir.dt.float32r
ACT = mybir.ActivationFunctionType
ALU = mybir.AluOpType
AX_X = mybir.AxisListType.X
P = 128

LN_EPS = 1e-5
RMS_EPS = 1e-6
LOWEST = -3.0e38


def wait_from(eng, sem, count):
    if not isinstance(count, int) or count > 0:
        eng.wait_ge(sem, count)


def waits_here(eng, passed):
    eng.sem_inc(passed, 1)


def bounds(total, size):
    return [(i, min(i + size, total)) for i in range(0, total, size)]


class Memory:

    def __init__(self, nc, ctx, stage):
        self.nc, self.ctx, self.stage = nc, ctx, stage

    def sbuf(self, name, shape, dtype=F32):
        return self.ctx.enter_context(self.nc.sbuf_tensor(f"{self.stage}_{name}", shape, dtype))

    def psum(self, name, shape, dtype=F32):
        return self.ctx.enter_context(self.nc.psum_tensor(f"{self.stage}_{name}", shape, dtype))

    def sem(self, name):
        return self.ctx.enter_context(self.nc.semaphore(f"{self.stage}_{name}"))


def query_stage(nc, d):
    B, S, D = d["x"].shape
    T = B * S
    NT = T // P
    GT = min(512, T)
    NG = T // GT
    GB = GT // S
    C = D // P
    NH = d["Wq"].shape[1] // P
    HQ = 4
    BAT = NH // HQ
    PAIRS = NH * S // P
    TPG = GT // P

    with ExitStack() as ctx:
        m = Memory(nc, ctx, "query")
        x_sb = m.sbuf("x", [P, NT, D])
        stats = m.sbuf("stats", [P, NT, 6])
        mv = m.sbuf("mv", [P, NT, 2])
        var = m.sbuf("var", [P, NT])
        rstd = m.sbuf("rstd", [P, NT])
        half = m.sbuf("half", [P, max(NT, B * PAIRS)])
        ident = m.sbuf("ident", [P, P])
        xn = m.sbuf("xn", [P, NT, D])
        xT_hi = m.sbuf("xT_hi", [P, C, T], F32R)
        xT_lo = m.sbuf("xT_lo", [P, C, T], F32R)
        w_raw = m.sbuf("w_raw", [P, C, NH * P])
        w_hi = m.sbuf("w_hi", [P, C, NH * P], F32R)
        w_lo = m.sbuf("w_lo", [P, C, NH * P], F32R)
        norm_w = m.sbuf("norm_w", [P, 2])
        wqk = m.sbuf("wqk", [P, 1])
        ones = m.sbuf("ones", [P, 1])
        qw = m.sbuf("qw", [P, 2, GB, HQ, S])
        sq = m.sbuf("sq", [P, 2, GB, HQ, S])
        msq = m.sbuf("msq", [P, B * PAIRS])
        rq = m.sbuf("rq", [P, B * PAIRS])
        tp = [m.psum(f"tp{i}", [P, GT]) for i in range(2)]
        qp = [m.psum(f"qp{i}", [P, GT]) for i in range(2)]
        ssq = m.psum("ssq", [P, B * PAIRS])

        loaded = m.sem("x_loaded")
        w_loaded = m.sem("w_loaded")
        w_split_hi = m.sem("w_split_hi")
        w_split_lo = m.sem("w_split_lo")
        const_ready = m.sem("const_ready")
        stats_ready = m.sem("stats_ready")
        mean_ready = m.sem("mean_ready")
        var_ready = m.sem("var_ready")
        rstd_ready = m.sem("rstd_ready")
        xn_ready = m.sem("xn_ready")
        tp_ready = m.sem("tp_ready")
        hi_ready = m.sem("hi_ready")
        lo_ready = m.sem("lo_ready")
        wqk_ready = m.sem("wqk_ready")
        q_ready = m.sem("q_ready")
        sq_ready = m.sem("sq_ready")
        qw_ready = m.sem("qw_ready")
        ssq_ready = m.sem("ssq_ready")
        qw_stored = [m.sem(f"qw_stored{i}") for i in range(2)]
        msq_ready = m.sem("msq_ready")
        rq_ready = m.sem("rq_ready")
        rq_stored = m.sem("rq_stored")
        passed = m.sem("passed")
        block = ctx.enter_context(nc.Block())
        XB = NG * C

        @block.sync
        def _(sp):
            sp.dma_start(x_sb[:], d["x"].rearrange("b s d -> (b s) d").rearrange(
                "(n p) d -> p n d", p=P)).then_inc(loaded, 16)
            sp.dma_start(w_raw[:], d["Wq"].rearrange("(c p) n -> p c n", p=P)).then_inc(w_loaded, 16)
            sp.dma_start(norm_w[:, 0:1], d["q_norm_w"].rearrange("(p a) -> p a", a=1)).then_inc(w_loaded, 16)
            sp.dma_start(norm_w[:, 1:2], d["k_norm_w"].rearrange("(p a) -> p a", a=1)).then_inc(w_loaded, 16)

            def group(g):
                for k in range(BAT):
                    sp.wait_ge(qw_ready, g * NH + (k + 1) * HQ)
                    waits_here(sp, passed)
                    sp.dma_start(
                        d["qT"][bass.ds(g * GB, GB), :, k * HQ:(k + 1) * HQ, :].rearrange("b p h s -> p b (h s)"),
                        qw[:, k % 2].rearrange("p b h s -> p b (h s)")).then_inc(qw_stored[k % 2], 16)

            with sp.Fori(0, NG) as g:
                group(g)
            sp.wait_ge(rq_ready, 1)
            sp.dma_start(d["rq"], rq[:]).then_inc(rq_stored, 16)
            for stored in qw_stored:
                sp.wait_ge(stored, 8 * NG * BAT)
            sp.wait_ge(rq_stored, 16)

        @block.gpsimd
        def _(pool):
            pool.memset(ident[:], 0.0).then_inc(const_ready, 1)
            pool.memset(ones[:], 1.0).then_inc(const_ready, 1)
            pool.memset(half[:], -0.5).then_inc(const_ready, 1)
            pool.wait_ge(const_ready, 3)
            pool.affine_select(out=ident[:], in_=ident[:], compare_op=ALU.not_equal, fill=1.0, base=0,
                               pattern=[[-1, P]], channel_multiplier=1).then_inc(const_ready, 1)
            pool.wait_ge(var_ready, 1)
            pool.tensor_tensor(rstd[:], var[:], half[:, 0:NT], ALU.pow).then_inc(rstd_ready, 1)
            pool.wait_ge(msq_ready, 1)
            pool.tensor_tensor(rq[:], msq[:], half[:, 0:B * PAIRS], ALU.pow).then_inc(rq_ready, 1)

        @block.vector
        def _(dve):
            dve.wait_ge(loaded, 16)
            for t in range(NT):
                dve.bn_stats(stats[:, t], x_sb[:, t]).then_inc(stats_ready, 1)
            for t in range(NT):
                dve.wait_ge(stats_ready, t + 1)
                dve.bn_aggr(mv[:, t], stats[:, t]).then_inc(mean_ready, 1)
            dve.wait_ge(mean_ready, NT)
            dve.tensor_scalar(var[:], mv[:, :, 1], LN_EPS, None, ALU.add).then_inc(var_ready, 1)
            dve.wait_ge(w_loaded, 48)
            dve.tensor_tensor(wqk[:], norm_w[:, 0:1], norm_w[:, 1:2], ALU.mult).then_inc(wqk_ready, 1)
            for c in range(C):
                dve.wait_ge(w_split_hi, c + 1)
                dve.tensor_tensor(w_lo[:, c], w_raw[:, c], w_hi[:, c], ALU.subtract).then_inc(w_split_lo, 1)
            dve.wait_ge(rstd_ready, 1)
            for t in range(NT):
                dve.tensor_scalar(xn[:, t], x_sb[:, t], mv[:, t, 0:1], rstd[:, t:t + 1],
                                  ALU.subtract, ALU.mult).then_inc(xn_ready, 1)
            for n in range(XB):
                g, c = n // C, n % C
                dve.wait_ge(hi_ready, n + 1)
                dve.tensor_tensor(xT_lo[:, c, g * GT:(g + 1) * GT], tp[n % 2][:],
                                  xT_hi[:, c, g * GT:(g + 1) * GT], ALU.subtract).then_inc(lo_ready, 1)
            dve.wait_ge(wqk_ready, 1)

            def group(g, first):
                for h in range(NH):
                    k, i = h // HQ, h % HQ
                    dve.wait_ge(sq_ready, g * NH + (h + 1))
                    if i == 0 and not (first and k < 2):
                        dve.wait_ge(qw_stored[k % 2], g * (8 * BAT) + 16 * (k // 2))
                    dve.tensor_scalar(qw[:, k % 2, :, i], qp[h % 2][:].rearrange("p (b s) -> p b s", s=S),
                                      wqk[:, 0:1], None, ALU.mult).then_inc(qw_ready, 1)

            group(0, True)
            if NG > 1:
                with dve.Fori(1, NG) as g:
                    group(g, False)
            dve.wait_ge(ssq_ready, NG * BAT)
            dve.tensor_scalar(msq[:], ssq[:], 1.0 / P, RMS_EPS, ALU.mult, ALU.add).then_inc(msq_ready, 1)

        @block.scalar
        def _(act):
            act.wait_ge(w_loaded, 48)
            for c in range(C):
                act.activation(w_hi[:, c], w_raw[:, c], ACT.Copy).then_inc(w_split_hi, 1)
            for n in range(XB):
                g, c = n // C, n % C
                act.wait_ge(tp_ready, n + 1)
                act.activation(xT_hi[:, c, g * GT:(g + 1) * GT], tp[n % 2][:], ACT.Copy).then_inc(hi_ready, 1)

            def group(g, first):
                for h in range(NH):
                    k, i = h // HQ, h % HQ
                    act.wait_ge(q_ready, g * NH + (h + 1))
                    if i == 0 and not (first and k < 2):
                        act.wait_ge(ssq_ready, g * BAT + (k - 1))
                    act.activation(sq[:, k % 2, :, i], qp[h % 2][:].rearrange("p (b s) -> p b s", s=S),
                                   ACT.Square).then_inc(sq_ready, 1)

            group(0, True)
            if NG > 1:
                with act.Fori(1, NG) as g:
                    group(g, False)

        @block.tensor
        def _(pe):
            pe.wait_ge(const_ready, 4)
            for n in range(XB):
                g, c = n // C, n % C
                pe.wait_ge(xn_ready, (g + 1) * TPG)
                if n >= 2:
                    pe.wait_ge(lo_ready, n - 1)
                for t in range(TPG):
                    last = pe.transpose(tp[n % 2][:, t * P:(t + 1) * P], xn[:, g * TPG + t, c * P:(c + 1) * P],
                                        ident[:])
                last.then_inc(tp_ready, 1)
            pe.wait_ge(lo_ready, XB)
            pe.wait_ge(w_split_lo, C)

            def squares(g, k):
                pe.wait_ge(sq_ready, g * NH + (k + 1) * HQ)
                for b in range(GB):
                    for j in range(HQ * S // P):
                        rows = sq[:, k % 2, b].rearrange("p h s -> p (h s)")[:, j * P:(j + 1) * P]
                        col = g * (GB * PAIRS) + (b * PAIRS + k * (HQ * S // P) + j)
                        last = pe.matmul(ssq[:, bass.ds(col, 1)], rows, ones[:, 0:1], start=True, stop=True,
                                         skip_group_check=True)
                last.then_inc(ssq_ready, 1)

            def group(g, first):
                for h in range(NH):
                    if not (first and h < 2):
                        pe.wait_ge(qw_ready, g * NH + (h - 1))
                    tok = bass.ds(g * GT, GT)
                    n = 0
                    for w, xs in ((w_hi, xT_hi), (w_hi, xT_lo), (w_lo, xT_hi)):
                        for c in range(C):
                            last = pe.matmul(qp[h % 2][:], w[:, c, h * P:(h + 1) * P], xs[:, c, tok],
                                             start=n == 0, stop=n == 3 * C - 1)
                            n += 1
                    last.then_inc(q_ready, 1)
                    if h % HQ == 0 and h:
                        squares(g, h // HQ - 1)
                squares(g, BAT - 1)

            group(0, True)
            if NG > 1:
                with pe.Fori(1, NG) as g:
                    group(g, False)


def attention_stage(nc, d):
    B, S, D = d["x"].shape
    KEYS = d["keys"]
    C = D // P
    KH = d["Wk"].shape[1] // P
    NH = d["Wq"].shape[1] // P
    QPK = NH // KH
    ROWS = QPK * S
    QT = ROWS // P
    PAIRS = NH * S // P
    PADDED = d["ctxT"].shape[3]
    TILES = bounds(PADDED, P)
    NT = len(TILES)
    SLOTS = [list(range(i, min(i + 2, NT))) for i in range(0, NT, 2)]
    NS = len(SLOTS)
    GROUPS = [list(range(i, min(i + 4, NT))) for i in range(0, NT, 4)]
    NGR = len(GROUPS)
    NC = 4
    piece = (PADDED // NC) // 2 * 2
    ends = [PADDED - piece * (NC - 1 - i) for i in range(NC)]
    CHUNKS = list(zip([0] + ends[:-1], ends))
    NSC = QT * NC
    SCORES = {0: [(0, 0), (1, 0)], 1: [(0, 1), (0, 2)], 2: [(1, 1), (0, 3)], 3: [(1, 2), (1, 3)]}
    COMPLETE = {2: 0, 3: 1}
    HALVES = bounds(KEYS, KEYS // 2 + 1)
    EXPS = {3: (0, 0), 4: (1, 0), 5: (0, 1), 6: (1, 1)}
    NE = len(EXPS)
    TURNED = {0: (0, 1), 1: (0, 2), 2: (0, 3), 5: (1, 0)}
    ORDER = [c for s in sorted(SCORES) for c in SCORES[s]]
    assert NS == 7 and NGR == 4 and QT == 2 and KH == 4

    def at(b, h, off, per, more):
        return b * (KH * per) + ((h + off) * per + more)

    def moved(b, h, off):
        return b * (KH // 2 * 16) + ((h + off) // 2 * 16 + 16)

    with ExitStack() as ctx:
        m = Memory(nc, ctx, "attn")
        c_raw = m.sbuf("c_raw", [P, C, PADDED])
        c_hi = m.sbuf("c_hi", [P, C, PADDED], F32R)
        c_lo = m.sbuf("c_lo", [P, C, PADDED], F32R)
        w_raw = m.sbuf("w_raw", [P, C, KH, 2, P])
        w_hi = m.sbuf("w_hi", [P, C, KH, 2 * P], F32R)
        w_lo = m.sbuf("w_lo", [P, C, KH, 2 * P], F32R)
        k_raw = m.sbuf("k_raw", [P, NT, P])
        k_sq = m.sbuf("k_sq", [P, 4, P])
        k_ss = m.sbuf("k_ss", [P, NT])
        k_ms = m.sbuf("k_ms", [P, NT])
        k_r = m.sbuf("k_r", [P, NT])
        k_unit = m.sbuf("k_unit", [P, 4, P])
        kT_hi = m.sbuf("kT_hi", [P, 2, NT * P], F32R)
        kT_lo = m.sbuf("kT_lo", [P, 2, NT * P], F32R)
        v_hi = m.sbuf("v_hi", [P, 2, NT, P], F32R)
        v_lo = m.sbuf("v_lo", [P, 2, NT, P], F32R)
        q_raw = m.sbuf("q_raw", [P, KH, ROWS])
        q_hi = m.sbuf("q_hi", [P, KH, ROWS], F32R)
        q_lo = m.sbuf("q_lo", [P, KH, ROWS], F32R)
        rq = m.sbuf("rq", [P, B * PAIRS])
        rqb = m.sbuf("rqb", [P, PAIRS])
        probs = m.sbuf("probs", [P, 2, QT, KEYS])
        pT = m.sbuf("pT", [P, 2, 2, 2, ROWS], F32R)
        piece_max = m.sbuf("piece_max", [P, QT, NC])
        row_max = m.sbuf("row_max", [P, QT])
        shift = m.sbuf("shift", [P, QT])
        den_parts = m.sbuf("den_parts", [P, 2, QT, 2])
        den = m.sbuf("den", [P, 2, QT])
        rden = m.sbuf("rden", [P, 2, QT])
        rden_b = m.sbuf("rden_b", [P, 2, ROWS])
        half_sum = m.sbuf("half_sum", [P, ROWS])
        oT = m.sbuf("oT", [P, 2, ROWS])
        ident = m.sbuf("ident", [P, P])
        neg_half = m.sbuf("neg_half", [P, 4])
        eps = m.sbuf("eps", [P, 4])
        s_ps = [m.psum(f"s{i}", [P, 512]) for i in range(2)]
        kv_ps = [m.psum(f"kv{i}", [P, 2, 2 * P]) for i in range(2)]
        pT_ps = [m.psum(f"pT{i}", [P, 2, ROWS]) for i in range(2)]
        kT_ps = m.psum("kT_ps", [P, 4 * P])
        o_ps = m.psum("o_ps", [P, 2, ROWS])

        consts = m.sem("consts")
        w_loaded = m.sem("w_loaded")
        w_hi_ready = m.sem("w_hi_ready")
        w_lo_ready = m.sem("w_lo_ready")
        c_loaded = m.sem("c_loaded")
        c_hi_ready = m.sem("c_hi_ready")
        c_lo_ready = m.sem("c_lo_ready")
        q_loaded = m.sem("q_loaded")
        q_hi_ready = m.sem("q_hi_ready")
        q_lo_ready = m.sem("q_lo_ready")
        rqb_ready = m.sem("rqb_ready")
        kv_ready = m.sem("kv_ready")
        v_hi_ready = m.sem("v_hi_ready")
        k_copied = m.sem("k_copied")
        v_lo_ready = m.sem("v_lo_ready")
        k_squared = m.sem("k_squared")
        k_summed = m.sem("k_summed")
        k_mean = m.sem("k_mean")
        k_r_ready = m.sem("k_r_ready")
        k_unit_ready = m.sem("k_unit_ready")
        kT_ready = m.sem("kT_ready")
        kT_hi_ready = m.sem("kT_hi_ready")
        kT_lo_ready = m.sem("kT_lo_ready")
        s_ready = m.sem("s_ready")
        s_copied = m.sem("s_copied")
        max_ready = m.sem("max_ready")
        shift_ready = m.sem("shift_ready")
        exp_ready = m.sem("exp_ready")
        den_ready = m.sem("den_ready")
        rden_ready = m.sem("rden_ready")
        rden_stored = m.sem("rden_stored")
        rden_b_ready = [m.sem(f"rden_b_ready{i}") for i in range(2)]
        pT_ready = m.sem("pT_ready")
        pT_hi_ready = m.sem("pT_hi_ready")
        pT_lo_ready = m.sem("pT_lo_ready")
        pv_done = m.sem("pv_done")
        half_ready = m.sem("half_ready")
        o_ready = m.sem("o_ready")
        o_stored = [m.sem(f"o_stored{i}") for i in range(2)]
        passed = m.sem("passed")
        block = ctx.enter_context(nc.Block())

        def pipeline(eng, step):
            step(-1, KH - 1, False, False, True)
            step(0, 0, True, False, True)
            for h in range(1, KH):
                step(0, h, True, True, h < KH - 1 or B > 1)
            if B > 2:
                with eng.Fori(1, B - 1) as b:
                    for h in range(KH):
                        step(b, h, True, True, True)
            if B > 1:
                for h in range(KH):
                    step(B - 1, h, True, True, h < KH - 1)
            step(B, 0, False, True, False)

        def j_bank(b, h, j):
            return ((h + 1) % 2 * NS + j) % 2

        def turned(b, h, j):
            off, i = (-1, j + 1) if j + 1 < NS else (0, 0)
            return off, i, ((h + off) % 2 * NS + i) % 2

        def s_bank(h, n):
            return s_ps[n % 2]

        def keys_of(tile):
            return min(TILES[tile][1], KEYS) - TILES[tile][0]

        def width(tiles):
            return TILES[tiles[-1]][1] - TILES[tiles[0]][0]

        def queries_after(b, h, scores, split):
            if scores and h == 0 and not (isinstance(b, int) and b == 0):
                split(b, KH - 1)
            if scores and h > 0 and not (isinstance(b, int) and b == B - 1):
                split(b + 1, h - 1)

        @block.sync
        def _(sp):
            for c in range(C):
                for n, w in enumerate((d["Wk"], d["Wv"])):
                    sp.dma_start(w_raw[:, c, :, n], w[c * P:(c + 1) * P, :].rearrange("p (h e) -> p h e", e=P)
                                 ).then_inc(w_loaded, 16)
            sp.dma_start(rq[:], d["rq"]).then_inc(w_loaded, 16)

            WEIGHTS = 16 * (2 * C + 1)

            def load_context(b):
                wait_from(sp, c_hi_ready, b * NS)
                wait_from(sp, c_lo_ready, b * NS)
                waits_here(sp, passed)
                sp.dma_start(c_raw[:], d["ctxT"][bass.ds(b, 1)].rearrange("a c p k -> (a p) c k")
                             ).then_inc(c_loaded, 16)

            def load_queries(b):
                wait_from(sp, q_lo_ready, b * KH)
                waits_here(sp, passed)
                sp.dma_start(q_raw[:].rearrange("p h r -> p (h r)"),
                             d["qT"][bass.ds(b, 1)].rearrange("a p h s -> (a p) (h s)")).then_inc(q_loaded, 16)

            load_context(0)
            load_queries(0)

            def step(b, h, scores, values, project):
                if scores and not (isinstance(b, int) and b == B - 1):
                    if h == 0:
                        load_context(b + 1)
                    if h == 1:
                        load_queries(b + 1)
                if scores:
                    sp.wait_ge(rden_ready, at(b, h, 0, 1, 1))
                    waits_here(sp, passed)
                    with nc.allow_non_contiguous_dma("256 numbers, a column each of two"):
                        sp.dma_start(d["rden"][bass.ds(b * KH + h, 1)].rearrange("u q p -> p (u q)"),
                                     rden[:, h % 2]).then_inc(rden_stored, 16)
                    sp.wait_ge(rden_stored, at(b, h, 0, 16, 16))
                    waits_here(sp, passed)
                    wait_from(sp, o_ready, at(b, h, 0, 1, -1))
                    waits_here(sp, passed)
                    sp.dma_start(rden_b[:, h % 2], d["rden"][bass.ds(b * KH + h, 1)].rearrange(
                        "u q p -> u (q p)").broadcast_to([P, ROWS])).then_inc(rden_b_ready[h % 2], 16)
                if values:
                    store_output(b, h)

            def store_output(b, h):
                hh = (h - 1) % KH
                bb = b if h > 0 else b - 1
                sp.wait_ge(o_ready, at(b, h, -1, 1, 1))
                waits_here(sp, passed)
                sp.dma_start(d["oT"][bass.ds(bb, 1), :, hh * QPK:(hh + 1) * QPK, :].rearrange(
                    "a p h s -> (a p) (h s)"), oT[:, hh % 2]).then_inc(o_stored[hh % 2], 16)

            pipeline(sp, step)
            for stored in o_stored:
                sp.wait_ge(stored, 8 * KH * B)

        @block.gpsimd
        def _(pool):
            pool.memset(ident[:], 0.0).then_inc(consts, 1)
            pool.memset(neg_half[:], -0.5).then_inc(consts, 1)
            pool.memset(eps[:], P * RMS_EPS).then_inc(consts, 1)
            pool.wait_ge(consts, 3)
            pool.affine_select(out=ident[:], in_=ident[:], compare_op=ALU.not_equal, fill=1.0, base=0,
                               pattern=[[-1, P]], channel_multiplier=1).then_inc(consts, 1)
            pool.wait_ge(consts, 4)

            def norms(b, h, g):
                tiles = GROUPS[g]
                n, rows = len(tiles), width(tiles[:1])
                sl = slice(tiles[0], tiles[-1] + 1)
                pool.wait_ge(k_copied, at(b, h, 1, NS, tiles[-1] // 2 + 1))
                wait_from(pool, k_summed, at(b, h, 1, NGR, g))
                pool.tensor_tensor(k_sq[:rows, 0:n], k_raw[:rows, sl], k_raw[:rows, sl], ALU.mult
                                   ).then_inc(k_squared, 1)
                pool.wait_ge(k_summed, at(b, h, 1, NGR, g + 1))
                pool.tensor_tensor(k_ms[:rows, sl], k_ss[:rows, sl], eps[:rows, 0:n], ALU.add
                                   ).then_inc(k_mean, 1)
                pool.wait_ge(k_mean, at(b, h, 1, NGR, g + 1))
                wait_from(pool, k_unit_ready, at(b, h, 0, NGR, g + 1))
                pool.tensor_tensor(k_r[:rows, sl], k_ms[:rows, sl], neg_half[:rows, 0:n], ALU.pow
                                   ).then_inc(k_r_ready, 1)
                pool.wait_ge(k_r_ready, at(b, h, 1, NGR, g + 1))
                wait_from(pool, kT_ready, at(b, h, 1, NGR, g))
                pool.tensor_tensor(k_unit[:rows, 0:n], k_raw[:rows, sl],
                                   k_r[:rows, sl].unsqueeze(2).broadcast_to([rows, n, P]), ALU.mult
                                   ).then_inc(k_unit_ready, 1)

            def split_queries(b, h):
                pool.wait_ge(q_hi_ready, at(b, h, 0, 1, 1))
                pool.tensor_tensor(q_lo[:, h], q_raw[:, h], q_hi[:, h], ALU.subtract).then_inc(q_lo_ready, 1)

            def step(b, h, scores, values, project):
                if isinstance(b, int) and b < 0:
                    for hh in range(KH):
                        split_queries(0, hh)
                for j in range(NS):
                    if project:
                        if j in (2, 4, 6):
                            norms(b, h, (j - 2) // 2)
                if project:
                    norms(b, h, 3)
                queries_after(b, h, scores, split_queries)

            pipeline(pool, step)

        @block.scalar
        def _(act):
            act.wait_ge(w_loaded, 16 * (2 * C + 1))
            for c in range(C):
                act.activation(w_hi[:, c], w_raw[:, c].rearrange("p h n e -> p h (n e)"), ACT.Copy
                               ).then_inc(w_hi_ready, 1)

            def split_context(b, j):
                a, z = TILES[SLOTS[j][0]][0], TILES[SLOTS[j][-1]][1]
                act.wait_ge(c_loaded, b * 16 + 16)
                wait_from(act, kv_ready, at(b, 0, -1, NS, NS + j + 1) - NS)
                act.activation(c_hi[:, :, a:z], c_raw[:, :, a:z], ACT.Copy).then_inc(c_hi_ready, 1)

            def split_queries(b, h):
                act.wait_ge(q_loaded, b * 16 + 16)
                wait_from(act, s_ready, at(b, h, -KH + 1, NSC, 0))
                act.activation(q_hi[:, h], q_raw[:, h], ACT.Copy).then_inc(q_hi_ready, 1)

            def exponentials(b, h, q, half):
                a, z = HALVES[half]
                act.wait_ge(shift_ready, at(b, h, 0, QT, q + 1))
                act.activation(probs[:, h % 2, q, a:z], probs[:, h % 2, q, a:z], ACT.Exp, bias=shift[:, q:q + 1],
                               scale=rqb[:, h * QT + q:h * QT + q + 1],
                               accum_out=den_parts[:, h % 2, q, half:half + 1]).then_inc(exp_ready, 1)

            def step(b, h, scores, values, project):
                first = isinstance(b, int) and b < 0
                if first:
                    for hh in range(KH):
                        split_queries(0, hh)
                    for j in range(NS):
                        split_context(0, j)
                for j in range(NS):
                    if scores if j == NS - 1 else values:
                        off, i, bank = turned(b, h, j)
                        n = len(SLOTS[i])
                        rows = keys_of(SLOTS[i][0])
                        act.wait_ge(pT_ready, at(b, h, off, NS, i + 1))
                        wait_from(act, pv_done, at(b, h, off, NS, i - 1))
                        act.activation(pT[:rows, bank, 0:n, 0], pT_ps[bank][:rows, 0:n], ACT.Copy
                                       ).then_inc(pT_hi_ready, 1)
                    if scores and j in EXPS:
                        exponentials(b, h, *EXPS[j])
                    if j in TURNED and (scores if TURNED[j][0] == 0 else project):
                        off, g = TURNED[j]
                        w = width(GROUPS[g])
                        a = TILES[GROUPS[g][0]][0]
                        act.wait_ge(kT_ready, at(b, h, off, NGR, g + 1))
                        wait_from(act, s_ready, at(b, h, off - 1, NSC, 0))
                        act.activation(kT_hi[:, (h + off) % 2, a:a + w], kT_ps[:, 0:w], ACT.Copy
                                       ).then_inc(kT_hi_ready, 1)
                    if project:
                        n = len(SLOTS[j])
                        rows = width(SLOTS[j][:1])
                        sl = slice(SLOTS[j][0], SLOTS[j][-1] + 1)
                        act.wait_ge(kv_ready, at(b, h, 1, NS, j + 1))
                        wait_from(act, pv_done, at(b, h, -1, NS, j + 1))
                        act.activation(v_hi[:rows, (h + 1) % 2, sl], kv_ps[j_bank(b, h, j)][:rows, 0:n, P:2 * P],
                                       ACT.Copy).then_inc(v_hi_ready, 1)
                        wait_from(act, k_unit_ready, at(b, h, 0, NGR, SLOTS[j][-1] // 4 + 1))
                        act.activation(k_raw[:rows, sl], kv_ps[j_bank(b, h, j)][:rows, 0:n, 0:P], ACT.Copy
                                       ).then_inc(k_copied, 1)
                    if project and h == KH - 2 and not (isinstance(b, int) and b == B - 1) and not first:
                        split_context(b + 1, j)
                queries_after(b, h, scores, split_queries)

            pipeline(act, step)

        @block.vector
        def _(dve):
            for c in range(C):
                dve.wait_ge(w_hi_ready, c + 1)
                dve.tensor_tensor(w_lo[:, c], w_raw[:, c].rearrange("p h n e -> p h (n e)"), w_hi[:, c],
                                  ALU.subtract).then_inc(w_lo_ready, 1)
            dve.wait_ge(w_loaded, 16 * (2 * C + 1))

            def split_context(b, j):
                a, z = TILES[SLOTS[j][0]][0], TILES[SLOTS[j][-1]][1]
                dve.wait_ge(c_hi_ready, b * NS + (j + 1))
                dve.tensor_tensor(c_lo[:, :, a:z], c_raw[:, :, a:z], c_hi[:, :, a:z], ALU.subtract
                                  ).then_inc(c_lo_ready, 1)

            def sum_squares(b, h, off, g):
                tiles = GROUPS[g]
                n, rows = len(tiles), width(tiles[:1])
                sl = slice(tiles[0], tiles[-1] + 1)
                dve.wait_ge(k_squared, at(b, h, off, NGR, g + 1))
                wait_from(dve, k_mean, at(b, h, off - 1, NGR, g + 1))
                dve.tensor_reduce(k_ss[:rows, sl], k_sq[:rows, 0:n], AX_X, ALU.add).then_inc(k_summed, 1)

            def add_halves(b, h):
                dve.wait_ge(pv_done, at(b, h, -1, NS, NS))
                wait_from(dve, o_ready, at(b, h, -1, 1, 0))
                dve.tensor_copy(half_sum[:], o_ps[:, 0]).then_inc(half_ready, 1)
                dve.wait_ge(half_ready, at(b, h, -1, 2, 1))
                dve.tensor_tensor(half_sum[:], o_ps[:, 1], half_sum[:], ALU.add).then_inc(half_ready, 1)

            def denominators(b, h):
                par = (h - 1) % 2
                dve.wait_ge(exp_ready, at(b, h, -1, NE, NE))
                dve.tensor_tensor(den[:, par], den_parts[:, par, :, 0], den_parts[:, par, :, 1],
                                  ALU.add).then_inc(den_ready, 1)
                dve.wait_ge(den_ready, at(b, h, -1, 1, 1))
                wait_from(dve, rden_stored, at(b, h, -1, 16, -16))
                dve.reciprocal(rden[:, par], den[:, par]).then_inc(rden_ready, 1)

            def output(b, h):
                par = (h - 1) % 2
                dve.wait_ge(half_ready, at(b, h, -1, 2, 2))
                dve.wait_ge(rden_b_ready[par], moved(b, h, -1))
                wait_from(dve, o_stored[par], moved(b, h, -3))
                dve.tensor_tensor(oT[:, par], half_sum[:], rden_b[:, par], ALU.mult).then_inc(o_ready, 1)

            def copy_scores(b, h, q, c):
                n = ORDER.index((q, c))
                a, z = CHUNKS[c]
                z = min(z, KEYS)
                dve.wait_ge(s_ready, at(b, h, 0, NSC, n + 1))
                if n == 0:
                    wait_from(dve, pT_ready, at(b, h, -1, NS, 0))
                    wait_from(dve, max_ready, at(b, h, 0, QT, 0))
                dve.tensor_scalar(probs[:, h % 2, q, a:z], s_bank(h, n)[:, 0:z - a], 1.0, LOWEST,
                                  ALU.mult, ALU.max, accum_out=piece_max[:, q, c:c + 1]
                                  ).then_inc(s_copied, 1)

            def step(b, h, scores, values, project):
                first = isinstance(b, int) and b < 0
                if first:
                    for j in range(NS):
                        split_context(0, j)
                for j in range(NS):
                    if scores and j == 0 and h == 0:
                        wait_from(dve, exp_ready, at(b, 0, 0, NE, 0))
                        dve.tensor_copy(rqb[:], rq[:, bass.ds(b * PAIRS, PAIRS)]).then_inc(rqb_ready, 1)
                    if scores if j == NS - 1 else values:
                        off, i, bank = turned(b, h, j)
                        n = len(SLOTS[i])
                        rows = keys_of(SLOTS[i][0])
                        dve.wait_ge(pT_hi_ready, at(b, h, off, NS, i + 1))
                        dve.tensor_tensor(pT[:rows, bank, 0:n, 1], pT_ps[bank][:rows, 0:n], pT[:rows, bank, 0:n, 0],
                                          ALU.subtract).then_inc(pT_lo_ready, 1)
                    if values and j == NS - 1:
                        add_halves(b, h)
                    if scores and j in SCORES:
                        copy_scores(b, h, *SCORES[j][0])
                    if j in TURNED and (scores if TURNED[j][0] == 0 else project):
                        off, g = TURNED[j]
                        w = width(GROUPS[g])
                        a = TILES[GROUPS[g][0]][0]
                        par = (h + off) % 2
                        dve.wait_ge(kT_hi_ready, at(b, h, off, NGR, g + 1))
                        dve.tensor_tensor(kT_lo[:, par, a:a + w], kT_ps[:, 0:w], kT_hi[:, par, a:a + w],
                                          ALU.subtract).then_inc(kT_lo_ready, 1)
                    if project:
                        n = len(SLOTS[j])
                        rows = width(SLOTS[j][:1])
                        sl = slice(SLOTS[j][0], SLOTS[j][-1] + 1)
                        dve.wait_ge(k_copied, at(b, h, 1, NS, j + 1))
                        dve.tensor_tensor(v_lo[:rows, (h + 1) % 2, sl], kv_ps[j_bank(b, h, j)][:rows, 0:n, P:2 * P],
                                          v_hi[:rows, (h + 1) % 2, sl], ALU.subtract).then_inc(v_lo_ready, 1)
                    if scores and j in SCORES:
                        copy_scores(b, h, *SCORES[j][1])
                    if scores and j in COMPLETE:
                        q = COMPLETE[j]
                        dve.wait_ge(s_copied, at(b, h, 0, NSC, 1 + max(i for i, c in enumerate(ORDER) if c[0] == q)))
                        dve.wait_ge(rqb_ready, b + 1)
                        dve.tensor_reduce(row_max[:, q:q + 1], piece_max[:, q], AX_X, ALU.max).then_inc(max_ready, 1)
                        dve.wait_ge(max_ready, at(b, h, 0, QT, q + 1))
                        wait_from(dve, exp_ready, at(b, h, 0, NE, 0))
                        dve.tensor_scalar(shift[:, q:q + 1], row_max[:, q:q + 1],
                                          rqb[:, h * QT + q:h * QT + q + 1], -1.0, ALU.mult, ALU.mult
                                          ).then_inc(shift_ready, 1)
                    if project and h == KH - 2 and not (isinstance(b, int) and b == B - 1) and not first:
                        split_context(b + 1, j)
                    if values and j == 0:
                        denominators(b, h)
                    if scores and j == 0:
                        sum_squares(b, h, 0, 3)
                    if project and j in (2, 4, 6):
                        sum_squares(b, h, 1, (j - 2) // 2)
                    if values and j == NS - 1:
                        output(b, h)

            pipeline(dve, step)

        @block.tensor
        def _(pe):
            pe.wait_ge(consts, 4)
            pe.wait_ge(w_lo_ready, C)

            def project_slot(b, h, j):
                hh = (h + 1) % KH
                bank = kv_ps[j_bank(b, h, j)]
                if hh == 0:
                    pe.wait_ge(c_lo_ready, (b + 1) * NS + (j + 1))
                wait_from(pe, v_lo_ready, at(b, h, 1, NS, j - 1))
                for i, t in enumerate(SLOTS[j]):
                    a, z = TILES[t]
                    n = 0
                    for cs, w in ((c_hi, w_hi), (c_hi, w_lo), (c_lo, w_hi)):
                        for c in range(C):
                            last = pe.matmul(bank[:z - a, i], cs[:, c, a:z], w[:, c, hh], start=n == 0,
                                             stop=n == 3 * C - 1)
                            n += 1
                last.then_inc(kv_ready, 1)

            def score_piece(b, h, q, c):
                n = ORDER.index((q, c))
                a, z = CHUNKS[c]
                groups = 1 + max(t for t in range(NT) if TILES[t][0] < z) // 4
                pe.wait_ge(kT_lo_ready, at(b, h, 0, NGR, groups))
                pe.wait_ge(q_lo_ready, at(b, h, 0, 1, 1))
                wait_from(pe, s_copied, at(b, h, 0, NSC, n - 1))
                for i, (x, y) in enumerate(((q_hi, kT_hi), (q_hi, kT_lo), (q_lo, kT_hi))):
                    last = pe.matmul(s_bank(h, n)[:, 0:z - a], x[:, h, q * P:(q + 1) * P], y[:, h % 2, a:z],
                                     start=i == 0, stop=i == 2)
                last.then_inc(s_ready, 1)

            def turn_keys(b, h, off, g):
                pe.wait_ge(k_unit_ready, at(b, h, off, NGR, g + 1))
                wait_from(pe, kT_lo_ready, at(b, h, off, NGR, g))
                for i, t in enumerate(GROUPS[g]):
                    a, z = TILES[t]
                    last = pe.transpose(kT_ps[:, i * P:i * P + z - a], k_unit[:z - a, i], ident[:z - a, :z - a])
                last.then_inc(kT_ready, 1)

            def turn_probs(b, h, j):
                off, slot, bank = turned(b, h, j)
                behind = TILES[SLOTS[slot][-1]][1] > HALVES[0][1]
                pe.wait_ge(exp_ready, at(b, h, off, NE, NE if behind else NE // 2))
                wait_from(pe, pT_lo_ready, at(b, h, off, NS, slot - 1))
                par = (h + off) % 2
                for i, t in enumerate(SLOTS[slot]):
                    a = TILES[t][0]
                    n = keys_of(t)
                    for q in range(QT):
                        last = pe.transpose(pT_ps[bank][:n, i, q * P:(q + 1) * P], probs[:, par, q, a:a + n],
                                            ident[:])
                last.then_inc(pT_ready, 1)

            def add_values(b, h, j):
                par = (h - 1) % 2
                bank = (par * NS + j) % 2
                pe.wait_ge(pT_lo_ready, at(b, h, -1, NS, j + 1))
                pe.wait_ge(v_lo_ready, at(b, h, -1, NS, j + 1))
                if j == 0:
                    wait_from(pe, half_ready, at(b, h, -1, 2, 0))
                for i, t in enumerate(SLOTS[j]):
                    n = keys_of(t)
                    pe.matmul(o_ps[:].rearrange("p a r -> p (a r)"), v_hi[:n, par, t],
                              pT[:n, bank, i].rearrange("p a r -> p (a r)"), start=t == 0, stop=False,
                              skip_group_check=True)
                    last = pe.matmul(o_ps[:, 0], v_lo[:n, par, t], pT[:n, bank, i, 0], start=False,
                                     stop=t == NT - 1, skip_group_check=True)
                last.then_inc(pv_done, 1)

            def step(b, h, scores, values, project):
                for j in range(NS):
                    if scores if j == NS - 1 else values:
                        turn_probs(b, h, j)
                    if scores and j in SCORES:
                        score_piece(b, h, *SCORES[j][0])
                    if j in TURNED and (scores if TURNED[j][0] == 0 else project):
                        turn_keys(b, h, *TURNED[j])
                    if values:
                        add_values(b, h, j)
                    if project:
                        project_slot(b, h, j)
                    if scores and j in SCORES:
                        score_piece(b, h, *SCORES[j][1])

            pipeline(pe, step)


def recurrent_stage(nc, d):
    B, S, D = d["x"].shape
    T = B * S
    C = D // P
    NH = d["Wo"].shape[0] // P
    GT = min(512, T)
    GB = GT // S
    NG = T // GT
    NT = GT // P
    BT = P // S
    E = d["experts"]
    TOP = d["top"]
    CAP = d["capacity"]
    SLOTS = E * CAP
    N_IN = 6

    with ExitStack() as ctx:
        m = Memory(nc, ctx, "rec")
        wo = m.sbuf("wo", [P, NH, D])
        w_in = m.sbuf("w_in", [P, N_IN, C, D])
        w_ro = m.sbuf("w_ro", [P, C, D])
        w_down = m.sbuf("w_down", [P, C, D])
        init = m.sbuf("init", [P, C])
        router = m.sbuf("router", [P, C, E])
        oT = m.sbuf("oT", [P, 2, NH, BT, S])
        x = m.sbuf("x", [P, NT, D])
        x1 = m.sbuf("x1", [P, NT, D])
        x2 = m.sbuf("x2", [P, NT, D])
        xn = m.sbuf("xn", [P, NT, D])
        xT = m.sbuf("xT", [P, C, GT])
        stats = m.sbuf("stats", [P, NT, 6])
        mv = m.sbuf("mv", [P, NT, 2])
        var = m.sbuf("var", [P, NT])
        rstd = m.sbuf("rstd", [P, NT])
        neg_half = m.sbuf("neg_half", [P, NT])
        f = m.sbuf("f", [P, C, GT])
        g_ = m.sbuf("g", [P, C, GT])
        sv = m.sbuf("sv", [P, C, GT])
        states = m.sbuf("states", [P, C, GT])
        z = m.sbuf("z", [P, C, GT])
        sz = m.sbuf("sz", [P, C, GT])
        mlp = m.sbuf("mlp", [P, C, GT])
        ident = m.sbuf("ident", [P, P])
        before = m.sbuf("before", [P, P])
        ones = m.sbuf("ones", [P, P])
        slot_base = m.sbuf("slot_base", [P, E])
        top_logit = m.sbuf("top_logit", [P, NT])
        expd = m.sbuf("expd", [P, NT, E])
        esum = m.sbuf("esum", [P, NT])
        resum = m.sbuf("resum", [P, NT])
        probs = m.sbuf("probs", [P, NT, E])
        top8 = m.sbuf("top8", [P, NT, 8])
        rest = m.sbuf("rest", [P, NT, E])
        chosen = m.sbuf("chosen", [P, NT, E])
        taken = m.sbuf("taken", [P, E])
        tmp = m.sbuf("tmp", [P, NT, E])
        kept = m.sbuf("kept", [P, NT, E])
        code = m.sbuf("code", [P, NT, E])
        code8 = m.sbuf("code8", [P, NT, TOP])
        same = m.sbuf("same", [P, NT, TOP, E])
        place = m.sbuf("place", [P, NT, TOP], mybir.dt.int32)
        pair = m.sbuf("pair", [P, NT, TOP, 2])
        token = m.sbuf("token", [P, NT])
        zero = m.sbuf("zero", [P, NT * D])
        empty = m.sbuf("empty", [P, E, 2])
        y_ps = [m.psum(f"y{i}", [P, 512]) for i in range(2)]
        in_ps = [m.psum(f"in{i}", [P, GT]) for i in range(3)]
        t_ps = m.psum("t", [P, GT])
        l_ps = m.psum("l", [P, NT, E])
        n_ps = m.psum("n", [P, NT, E])

        w_loaded = m.sem("w_loaded")
        consts = m.sem("consts")
        tables_set = m.sem("tables_set")
        o_loaded = [m.sem(f"o_loaded{i}") for i in range(2)]
        x_loaded = m.sem("x_loaded")
        y_ready = m.sem("y_ready")
        x1_ready = m.sem("x1_ready")
        chain = m.sem("dve_step")
        var_ready = m.sem("var_ready")
        rstd_ready = m.sem("rstd_ready")
        xn_ready = m.sem("xn_ready")
        turned = m.sem("turned")
        xT_ready = m.sem("xT_ready")
        in_ready = m.sem("in_ready")
        act_in = m.sem("act_in")
        read_by_dve = m.sem("read_by_dve")
        gated = m.sem("gated")
        z_ready = m.sem("z_ready")
        sz_ready = m.sem("sz_ready")
        mixed = m.sem("mixed")
        out_ready = m.sem("out_ready")
        x2_ready = m.sem("x2_ready")
        x2_stored = m.sem("x2_stored")
        xn_stored = m.sem("xn_stored")
        logits = m.sem("logits")
        top_ready = m.sem("top_ready")
        exp_ready = m.sem("exp_ready")
        chosen_ready = m.sem("chosen_ready")
        counted = m.sem("counted")
        pair_ready = m.sem("pair_ready")
        scattered = m.sem("scattered")
        passed = m.sem("passed")
        block = ctx.enter_context(nc.Block())

        W_F, W_I, W_V, W_GATE, W_UP, W_Q = range(N_IN)
        FILLS = ([(w, c) for c in range(C) for w in (W_F, W_I, W_V)]
                 + [(w, c) for c in range(C) for w in (W_GATE, W_UP)] + [(W_Q, c) for c in range(C)])
        NF = len(FILLS)
        BY_ACT = [n for n, (w, _) in enumerate(FILLS) if w in (W_F, W_I, W_V, W_GATE)]
        BY_DVE = [n for n, (w, _) in enumerate(FILLS) if w in (W_V, W_GATE, W_UP)]

        def groups(eng, body):
            body(0)
            if NG > 1:
                with eng.Fori(1, NG) as g:
                    body(g)

        @block.sync
        def _(sp):
            sp.dma_start(wo[:], d["Wo"].rearrange("(h p) n -> p h n", p=P)).then_inc(w_loaded, 16)
            for n, name in ((W_F, "w_f"), (W_I, "w_i"), (W_V, "w_v"), (W_Q, "w_q"), (W_UP, "w_up"), (W_GATE, "w_gate")):
                sp.dma_start(w_in[:, n], d[name].rearrange("(c p) n -> p c n", p=P)).then_inc(w_loaded, 16)
            sp.dma_start(w_ro[:], d["w_ro"].rearrange("(c p) n -> p c n", p=P)).then_inc(w_loaded, 16)
            sp.dma_start(w_down[:], d["w_down"].rearrange("(c p) n -> p c n", p=P)).then_inc(w_loaded, 16)
            with nc.allow_non_contiguous_dma("256 numbers"):
                sp.dma_start(init[:], d["init_state"].rearrange("(c p) -> p c", p=P)).then_inc(w_loaded, 16)
            sp.dma_start(router[:], d["routerT"].rearrange("(c p) e -> p c e", p=P)).then_inc(w_loaded, 16)
            sp.wait_ge(consts, 9)
            sp.dma_start(d["tokens"][T:T + P, :], zero[:, 0:D]).then_inc(tables_set, 16)
            sp.dma_start(d["slots"].rearrange("(p e) w -> p e w", e=E), empty[:CAP]).then_inc(tables_set, 16)
            sp.dma_start(d["sum0"][T:T + P, :], zero[:, 0:D]).then_inc(tables_set, 16)
            sp.dma_start(d["sum1"][T:T + P, :], zero[:, 0:D]).then_inc(tables_set, 16)
            for g in range(NG):
                sp.dma_start(d["sum1"][g * GT:(g + 1) * GT, :].rearrange("(p r) d -> p (r d)", p=P), zero[:]
                             ).then_inc(tables_set, 16)
            sp.wait_ge(tables_set, 16 * (4 + NG))

            def load(g):
                if not isinstance(g, int):
                    sp.wait_ge(x1_ready, g * NT)
                    waits_here(sp, passed)
                sp.dma_start(x[:], d["x"][bass.ds(g * GB, GB)].rearrange("b s d -> (b s) d").rearrange(
                    "(n p) d -> p n d", p=P)).then_inc(x_loaded, 16)
                for t in range(NT):
                    wait_from(sp, y_ready, g * NT + (t - 1))
                    waits_here(sp, passed)
                    for b in range(BT):
                        sp.dma_start(oT[:, t % 2, :, b], d["oT"][bass.ds(g * GB + t * BT + b, 1)].rearrange(
                            "a p h s -> (a p) h s")).then_inc(o_loaded[t % 2], 16)

            def body(g):
                load(g)
                sp.wait_ge(x2_ready, g * NT + NT)
                waits_here(sp, passed)
                sp.dma_start(d["sum0"][bass.ds(g * GT, GT)].rearrange("(n p) d -> p n d", p=P), x2[:]
                             ).then_inc(x2_stored, 16)
                sp.wait_ge(xn_ready, g * (2 * NT) + 2 * NT)
                waits_here(sp, passed)
                sp.dma_start(d["tokens"][bass.ds(g * GT, GT)].rearrange("(n p) d -> p n d", p=P), xn[:]
                             ).then_inc(xn_stored, 16)

            groups(sp, body)
            sp.wait_ge(x2_stored, 16 * NG)
            sp.wait_ge(xn_stored, 16 * NG)

        @block.gpsimd
        def _(pool):
            pool.memset(ident[:], 0.0).then_inc(consts, 1)
            pool.memset(before[:], 1.0).then_inc(consts, 1)
            pool.memset(ones[:], 1.0).then_inc(consts, 1)
            pool.memset(neg_half[:], -0.5).then_inc(consts, 1)
            pool.memset(zero[:], 0.0).then_inc(consts, 1)
            pool.memset(empty[:], 0.0).then_inc(consts, 1)
            pool.wait_ge(consts, 6)
            pool.affine_select(out=ident[:], in_=ident[:], compare_op=ALU.not_equal, fill=1.0, base=0,
                               pattern=[[-1, P]], channel_multiplier=1).then_inc(consts, 1)
            pool.affine_select(out=before[:], in_=before[:], compare_op=ALU.is_gt, fill=0.0, base=0,
                               pattern=[[1, P]], channel_multiplier=-1).then_inc(consts, 1)
            pool.iota(empty[:, :, 1], [[0, E]], base=T, channel_multiplier=1,
                      allow_small_or_imprecise_dtypes=True).then_inc(consts, 1)
            pool.iota(slot_base[:], [[-1, E]], base=SLOTS, channel_multiplier=0,
                      allow_small_or_imprecise_dtypes=True).then_inc(consts, 1)
            pool.iota(token[:], [[P, NT]], base=0, channel_multiplier=1,
                      allow_small_or_imprecise_dtypes=True).then_inc(consts, 1)

            def body(g):
                for k in range(2):
                    pool.wait_ge(var_ready, g * 2 + (k + 1))
                    pool.tensor_tensor(rstd[:], var[:], neg_half[:], ALU.pow).then_inc(rstd_ready, 1)
                if isinstance(g, int):
                    pool.wait_ge(tables_set, 16 * (4 + NG))
                for t in range(NT):
                    pool.wait_ge(pair_ready, g * NT + (t + 1))
                    waits_here(pool, passed)
                    for k in range(TOP):
                        pool.indirect_dma_start(
                            out=d["slots"], out_offset=bass.IndirectOffsetOnAxis(ap=place[:, t, k:k + 1], axis=0),
                            in_=pair[:, t, k], in_offset=None, bounds_check=SLOTS - 1, oob_is_err=False
                        ).then_inc(scattered, 16)

            groups(pool, body)
            pool.wait_ge(scattered, 16 * NG * NT * TOP)

        @block.scalar
        def _(act):
            def body(g):
                for c in range(C):
                    act.wait_ge(turned, g * (2 * C) + (c + 1))
                    act.activation(xT[:, c], t_ps[:], ACT.Copy).then_inc(xT_ready, 1)
                for n in BY_ACT:
                    w, c = FILLS[n]
                    act.wait_ge(in_ready, g * NF + (n + 1))
                    out = {W_F: f, W_I: g_, W_V: sv, W_GATE: sv}[w]
                    if w == W_GATE:
                        act.wait_ge(gated, g * C + (c + 1))
                    act.activation(out[:, c], in_ps[n % 3][:], ACT.Tanh if w == W_F else ACT.Sigmoid
                                   ).then_inc(act_in, 1)
                for c in range(C):
                    act.wait_ge(z_ready, g * C + (c + 1))
                    act.activation(sz[:, c], z[:, c], ACT.Sigmoid).then_inc(sz_ready, 1)
                for c in range(C):
                    act.wait_ge(turned, g * (2 * C) + (C + c + 1))
                    act.activation(xT[:, c], t_ps[:], ACT.Copy).then_inc(xT_ready, 1)
                for t in range(NT):
                    act.wait_ge(top_ready, g + 1)
                    act.activation(expd[:, t], l_ps[:, t], ACT.Exp, bias=top_logit[:, t:t + 1],
                                   accum_out=esum[:, t:t + 1]).then_inc(exp_ready, 1)

            groups(act, body)

        @block.vector
        def _(dve):
            steps = [0]

            def body(g):
                steps[0] = 0

                def link(ins):
                    steps[0] += 1
                    ins.then_inc(chain, 1)
                    dve.wait_ge(chain, g * LINKS + steps[0])
                    waits_here(dve, passed)

                def norm(src, k):
                    for t in range(NT):
                        link(dve.bn_stats(stats[:, t], src[:, t]))
                        link(dve.bn_aggr(mv[:, t], stats[:, t]))
                    dve.tensor_scalar(var[:], mv[:, :, 1], LN_EPS, None, ALU.add).then_inc(var_ready, 1)
                    dve.wait_ge(rstd_ready, g * 2 + (k + 1))
                    if k == 0:
                        wait_from(dve, xn_stored, g * 16)
                    for t in range(NT):
                        dve.tensor_scalar(xn[:, t], src[:, t], mv[:, t, 0:1], rstd[:, t:t + 1],
                                          ALU.subtract, ALU.mult).then_inc(xn_ready, 1)

                dve.wait_ge(x_loaded, g * 16 + 16)
                for t in range(NT):
                    dve.wait_ge(y_ready, g * NT + (t + 1))
                    dve.tensor_tensor(x1[:, t], y_ps[t % 2][:, 0:D], x[:, t], ALU.add).then_inc(x1_ready, 1)
                dve.wait_ge(x1_ready, g * NT + NT)
                norm(x1, 0)
                for c in range(C):
                    n = c * 3 + 2
                    dve.wait_ge(act_in, g * len(BY_ACT) + (n + 1))
                    dve.tensor_tensor(sv[:, c], in_ps[n % 3][:], sv[:, c], ALU.mult).then_inc(read_by_dve, 1)
                    dve.wait_ge(read_by_dve, g * len(BY_DVE) + (c + 1))
                    dve.tensor_tensor(g_[:, c], g_[:, c], sv[:, c], ALU.mult).then_inc(gated, 1)
                    dve.wait_ge(gated, g * C + (c + 1))
                    fs = f[:, c].rearrange("p (b s) -> p b s", s=S)[:, :, 0]
                    gs = g_[:, c].rearrange("p (b s) -> p b s", s=S)[:, :, 0]
                    link(dve.scalar_tensor_tensor(out=gs, in0=fs, scalar=init[:, c:c + 1], in1=gs,
                                                  op0=ALU.mult, op1=ALU.add))
                    link(dve.memset(fs, 0.0))
                    link(dve.tensor_tensor_scan(states[:, c], f[:, c], g_[:, c], 0.0, ALU.mult, ALU.add))
                for c in range(C):
                    n = 3 * C + 2 * c
                    dve.wait_ge(act_in, g * len(BY_ACT) + (3 * C + c + 1))
                    dve.tensor_tensor(sv[:, c], in_ps[n % 3][:], sv[:, c], ALU.mult).then_inc(read_by_dve, 1)
                    dve.wait_ge(read_by_dve, g * len(BY_DVE) + (C + 2 * c + 1))
                    dve.wait_ge(in_ready, g * NF + (n + 2))
                    dve.tensor_tensor(mlp[:, c], in_ps[(n + 1) % 3][:], sv[:, c], ALU.mult
                                      ).then_inc(read_by_dve, 1)
                for c in range(C):
                    n = 5 * C + c
                    dve.wait_ge(in_ready, g * NF + (n + 1))
                    dve.tensor_tensor(z[:, c], in_ps[n % 3][:], states[:, c], ALU.mult).then_inc(z_ready, 1)
                for c in range(C):
                    dve.wait_ge(sz_ready, g * C + (c + 1))
                    dve.tensor_tensor(sz[:, c], z[:, c], sz[:, c], ALU.mult).then_inc(mixed, 1)
                wait_from(dve, x2_stored, g * 16)
                for t in range(NT):
                    dve.wait_ge(out_ready, g * NT + (t + 1))
                    dve.tensor_tensor(x2[:, t], y_ps[t % 2][:, 0:D], x1[:, t], ALU.add).then_inc(x2_ready, 1)
                dve.wait_ge(x2_ready, g * NT + NT)
                dve.wait_ge(turned, g * (2 * C) + C)
                norm(x2, 1)
                dve.wait_ge(logits, g * NT + NT)
                link(dve.tensor_reduce(top_logit[:], l_ps[:], AX_X, ALU.max))
                dve.tensor_scalar(top_logit[:], top_logit[:], -1.0, None, ALU.mult).then_inc(top_ready, 1)
                dve.wait_ge(exp_ready, g * NT + NT)
                link(dve.reciprocal(resum[:], esum[:]))
                link(dve.tensor_tensor(probs[:], expd[:], resum[:].unsqueeze(2).broadcast_to([P, NT, E]), ALU.mult))
                for t in range(NT):
                    link(dve.max(top8[:, t], probs[:, t]))
                    link(dve.match_replace(rest[:, t], top8[:, t], probs[:, t], -1.0))
                dve.tensor_scalar(chosen[:], rest[:], 0.0, None, ALU.is_lt).then_inc(chosen_ready, 1)
                dve.wait_ge(counted, g * NT + NT)
                link(dve.scalar_tensor_tensor(out=tmp[:], in0=n_ps[:], scalar=float(-E),
                                              in1=slot_base[:].unsqueeze(1).broadcast_to([P, NT, E]),
                                              op0=ALU.mult, op1=ALU.add))
                link(dve.scalar_tensor_tensor(out=kept[:], in0=n_ps[:], scalar=float(CAP), in1=chosen[:],
                                              op0=ALU.is_lt, op1=ALU.mult))
                link(dve.tensor_tensor(code[:], tmp[:], kept[:], ALU.mult))
                wait_from(dve, scattered, g * (16 * NT * TOP))
                waits_here(dve, passed)
                for t in range(NT):
                    link(dve.max(code8[:, t], code[:, t]))
                    link(dve.tensor_scalar(place[:, t], code8[:, t], -1.0, float(SLOTS), ALU.mult, ALU.add))
                    link(dve.tensor_tensor(same[:, t], code8[:, t].unsqueeze(2).broadcast_to([P, TOP, E]),
                                           code[:, t].unsqueeze(1).broadcast_to([P, TOP, E]), ALU.is_equal))
                    link(dve.tensor_tensor(same[:, t], same[:, t],
                                           probs[:, t].unsqueeze(1).broadcast_to([P, TOP, E]), ALU.mult))
                    link(dve.tensor_copy(pair[:, t, :, 1], token[:, t:t + 1].broadcast_to([P, TOP])))
                    dve.tensor_reduce(pair[:, t, :, 0], same[:, t], AX_X, ALU.add).then_inc(pair_ready, 1)
                for t in range(NT):
                    link(dve.tensor_tensor(taken[:], taken[:], chosen[:, t], ALU.add))
                link(dve.tensor_scalar(token[:], token[:], float(GT), None, ALU.add))

            LINKS = 12 * NT + 3 * C + 7
            dve.wait_ge(w_loaded, 16 * 11)
            dve.wait_ge(consts, 11)
            dve.memset(taken[:], 0.0).then_inc(consts, 1)
            dve.wait_ge(consts, 12)
            groups(dve, body)
            assert steps[0] == LINKS, steps[0]

        @block.tensor
        def _(pe):
            pe.wait_ge(w_loaded, 16 * 11)
            pe.wait_ge(consts, 12)

            def turn(g, k):
                pe.wait_ge(xn_ready, g * (2 * NT) + (k + 1) * NT)
                for c in range(C):
                    wait_from(pe, xT_ready, g * (2 * C) + (k * C + c))
                    for t in range(NT):
                        last = pe.transpose(t_ps[:, t * P:(t + 1) * P], xn[:, t, c * P:(c + 1) * P], ident[:])
                    last.then_inc(turned, 1)
                pe.wait_ge(xT_ready, g * (2 * C) + (k + 1) * C)

            def body(g):
                for t in range(NT):
                    pe.wait_ge(o_loaded[t % 2], g * (NT // 2 * BT * 16) + BT * 16 * (t // 2 + 1))
                    if t < 2:
                        wait_from(pe, x2_ready, g * NT)
                    else:
                        pe.wait_ge(x1_ready, g * NT + (t - 1))
                    for h in range(NH):
                        last = pe.matmul(y_ps[t % 2][:, 0:D], oT[:, t % 2, h].rearrange("p b s -> p (b s)"), wo[:, h], start=h == 0,
                                         stop=h == NH - 1)
                    last.then_inc(y_ready, 1)
                turn(g, 0)
                for n, (w, c) in enumerate(FILLS):
                    p = n - 3
                    if p >= 0:
                        if p in BY_DVE:
                            pe.wait_ge(read_by_dve, g * len(BY_DVE) + (BY_DVE.index(p) + 1))
                        else:
                            pe.wait_ge(act_in, g * len(BY_ACT) + (BY_ACT.index(p) + 1))
                    else:
                        wait_from(pe, z_ready, g * C)
                    for i in range(C):
                        last = pe.matmul(in_ps[n % 3][:], w_in[:, w, i, c * P:(c + 1) * P], xT[:, i], start=i == 0,
                                         stop=i == C - 1)
                    last.then_inc(in_ready, 1)
                pe.wait_ge(mixed, g * C + C)
                for t in range(NT):
                    if t >= 2:
                        pe.wait_ge(x2_ready, g * NT + (t - 1))
                    else:
                        pe.wait_ge(x1_ready, g * NT + NT)
                    n = 0
                    for a, w in ((sz, w_ro), (mlp, w_down)):
                        for c in range(C):
                            last = pe.matmul(y_ps[t % 2][:, 0:D], a[:, c, t * P:(t + 1) * P], w[:, c], start=n == 0,
                                             stop=n == 2 * C - 1)
                            n += 1
                    last.then_inc(out_ready, 1)
                turn(g, 1)
                wait_from(pe, exp_ready, g * NT)
                for t in range(NT):
                    for c in range(C):
                        last = pe.matmul(l_ps[:, t], xT[:, c, t * P:(t + 1) * P], router[:, c], start=c == 0,
                                         stop=c == C - 1)
                    last.then_inc(logits, 1)
                pe.wait_ge(chosen_ready, g + 1)
                for t in range(NT):
                    pe.matmul(n_ps[:, t], ones[:], taken[:], start=True, stop=False)
                    for i in range(t):
                        pe.matmul(n_ps[:, t], ones[:], chosen[:, i], start=False, stop=False)
                    pe.matmul(n_ps[:, t], before[:], chosen[:, t], start=False, stop=True).then_inc(counted, 1)

            groups(pe, body)


def expert_stage(nc, d):
    B, S, D = d["x"].shape
    T = B * S
    C = D // P
    E = d["experts"]
    NT = T // P
    F = d["w_gate"].shape[2]
    U = 8
    AHEAD = 5
    PIECES = 4
    assert F == P and E % U == 0 and E // U >= 2 and NT % PIECES == 0

    with ExitStack() as ctx:
        m = Memory(nc, ctx, "moe")
        pairs = m.sbuf("pairs", [P, E, 2])
        ids = m.sbuf("ids", [P, E], mybir.dt.int32)
        weight = m.sbuf("weight", [P, E])
        rows = m.sbuf("rows", [P, U], mybir.dt.int32)
        ident = m.sbuf("ident", [P, P])
        wg = m.sbuf("wg", [P, U, C, F])
        wu = m.sbuf("wu", [P, U, C, F])
        wd = m.sbuf("wd", [P, U, D])
        xg = m.sbuf("xg", [P, U, D])
        xT = m.sbuf("xT", [P, 2, C, P])
        sig = m.sbuf("sig", [P, 2, P])
        gate = m.sbuf("gate", [P, 2, P])
        hid = m.sbuf("hid", [P, 2, P])
        yw = m.sbuf("yw", [P, U, D])
        sums = m.sbuf("sums", [P, 2, NT, D])
        total = m.sbuf("total", [P, NT, D])
        t_ps = [m.psum(f"t{i}", [P, C, P]) for i in range(2)]
        gu_ps = [m.psum(f"gu{i}", [P, 2, P]) for i in range(2)]
        y_ps = [m.psum(f"y{i}", [P, D]) for i in range(2)]

        consts = m.sem("consts")
        pairs_loaded = m.sem("pairs_loaded")
        ids_ready = m.sem("ids_ready")
        rows_ready = m.sem("rows_ready")
        w_loaded = [m.sem(f"w_loaded{i}") for i in range(U // 2)]
        gathered = [m.sem(f"gathered{i}") for i in range(U)]
        turned = m.sem("turned")
        xT_ready = m.sem("xT_ready")
        gu_ready = m.sem("gu_ready")
        sig_ready = m.sem("sig_ready")
        gate_ready = m.sem("gate_ready")
        hid_ready = m.sem("hid_ready")
        y_ready = m.sem("y_ready")
        yw_ready = m.sem("yw_ready")
        added = [m.sem(f"added{i}") for i in range(2)]
        sums_loaded = [m.sem(f"sums_loaded{i}") for i in range(PIECES)]
        total_ready = m.sem("total_ready")
        stored = m.sem("stored")
        passed = m.sem("passed")
        block = ctx.enter_context(nc.Block())

        NP = NT // PIECES

        def experts(eng, body):
            body(0, False)
            if E > 2 * U:
                with eng.Fori(1, E // U - 1) as i:
                    body(i, False)
            body(E // U - 1, True)

        @block.sync
        def _(sp):
            sp.dma_start(pairs[:], d["slots"].rearrange("(p e) w -> p e w", e=E)).then_inc(pairs_loaded, 16)

            def body(i, last):
                for k in range(0, U, 2):
                    wait_from(sp, y_ready, i * U + (k - U + 2))
                    waits_here(sp, passed)
                    for buf, name in ((wg, "w_gate"), (wu, "w_up")):
                        sp.dma_start(buf[:, k:k + 2].rearrange("p e c f -> p (e c) f"),
                                     d[name][bass.ds(i * U + k, 2)].rearrange(
                                         "a (c p) f -> p (a c) f", p=P)).then_inc(w_loaded[k // 2], 16)
                    sp.dma_start(wd[:, k:k + 2], d["w_down"][bass.ds(i * U + k, 2)].rearrange(
                        "a p n -> p a n")).then_inc(w_loaded[k // 2], 16)

            experts(sp, body)
            for n in range(2):
                sp.wait_ge(added[n], 16 * (E // 2))
            for c in range(PIECES):
                for n in range(2):
                    sp.dma_start(sums[:, n, c * NP:(c + 1) * NP], d[f"sum{n}"][c * NP * P:(c + 1) * NP * P].rearrange(
                        "(n p) d -> p n d", p=P)).then_inc(sums_loaded[c], 16)
            for c in range(PIECES):
                sp.wait_ge(total_ready, c + 1)
                sp.dma_start(d["out"].rearrange("b s d -> (b s) d")[c * NP * P:(c + 1) * NP * P].rearrange(
                    "(n p) d -> p n d", p=P), total[:, c * NP:(c + 1) * NP]).then_inc(stored, 16)
            sp.wait_ge(stored, 16 * PIECES)

        @block.gpsimd
        def _(pool):
            pool.memset(ident[:], 0.0).then_inc(consts, 1)
            pool.wait_ge(consts, 1)
            pool.affine_select(out=ident[:], in_=ident[:], compare_op=ALU.not_equal, fill=1.0, base=0,
                               pattern=[[-1, P]], channel_multiplier=1).then_inc(consts, 1)
            pool.wait_ge(ids_ready, 1)
            last_row = pool.to_reg(T + P - 1)

            def gather(i, k):
                pool.tensor_copy(rows[:, k:k + 1], ids[:, bass.ds(i * U + k, 1)]).then_inc(rows_ready, 1)
                wait_from(pool, turned, i * U + (k - U + 1))
                pool.wait_ge(rows_ready, i * U + (k + 1))
                waits_here(pool, passed)
                pool.indirect_dma_start(out=xg[:, k], out_offset=None, in_=d["tokens"],
                                        in_offset=bass.IndirectOffsetOnAxis(ap=rows[:, k:k + 1], axis=0),
                                        bounds_check=last_row, oob_is_err=True).then_inc(gathered[k], 16)

            for k in range(AHEAD):
                gather(0, k)

            def body(i, last):
                for k in range(U):
                    if not (last and k + AHEAD >= U):
                        gather(i + (k + AHEAD) // U, (k + AHEAD) % U)
                    pool.wait_ge(yw_ready, i * U + (k + 1))
                    wait_from(pool, added[k % 2], i * (U // 2 * 16) + k // 2 * 16)
                    waits_here(pool, passed)
                    pool.indirect_dma_start(out=d[f"sum{k % 2}"],
                                            out_offset=bass.IndirectOffsetOnAxis(ap=rows[:, k:k + 1], axis=0),
                                            in_=yw[:, k], in_offset=None, bounds_check=last_row,
                                            oob_is_err=True, compute_op=ALU.add).then_inc(added[k % 2], 16)

            experts(pool, body)

        @block.scalar
        def _(act):
            def columns(i, k):
                act.wait_ge(turned, i * U + (k + 1))
                wait_from(act, gu_ready, i * U + (k - 1))
                act.activation(xT[:, k % 2], t_ps[k % 2][:], ACT.Copy).then_inc(xT_ready, 1)

            def sigmoid(i, k):
                act.wait_ge(gu_ready, i * U + (k + 1))
                act.activation(sig[:, k % 2], gu_ps[k % 2][:, 0], ACT.Sigmoid).then_inc(sig_ready, 1)

            def body(i, last):
                for k in range(U):
                    if not (last and k + 2 >= U):
                        columns(i + (k + 2) // U, (k + 2) % U)
                    if not (last and k + 1 >= U):
                        sigmoid(i + (k + 1) // U, (k + 1) % U)
                    act.wait_ge(y_ready, i * U + (k + 1))
                    wait_from(act, added[k % 2], i * (U // 2 * 16) + (k // 2 - U // 2 + 1) * 16)
                    act.activation(yw[:, k], y_ps[k % 2][:], ACT.Copy, scale=weight[:, bass.ds(i * U + k, 1)]
                                   ).then_inc(yw_ready, 1)

            columns(0, 0)
            columns(0, 1)
            sigmoid(0, 0)
            act.wait_ge(ids_ready, 2)
            experts(act, body)

        @block.vector
        def _(dve):
            dve.wait_ge(pairs_loaded, 16)
            dve.tensor_copy(ids[:], pairs[:, :, 1]).then_inc(ids_ready, 1)
            dve.tensor_copy(weight[:], pairs[:, :, 0]).then_inc(ids_ready, 1)

            def body(i, last):
                for k in range(U):
                    dve.wait_ge(sig_ready, i * U + (k + 1))
                    dve.tensor_tensor(gate[:, k % 2], gu_ps[k % 2][:, 0], sig[:, k % 2], ALU.mult
                                      ).then_inc(gate_ready, 1)
                    dve.wait_ge(gate_ready, i * U + (k + 1))
                    dve.tensor_tensor(hid[:, k % 2], gu_ps[k % 2][:, 1], gate[:, k % 2], ALU.mult
                                      ).then_inc(hid_ready, 1)

            experts(dve, body)
            for c in range(PIECES):
                dve.wait_ge(sums_loaded[c], 32)
                sl = slice(c * NP, (c + 1) * NP)
                dve.tensor_tensor(total[:, sl], sums[:, 0, sl], sums[:, 1, sl], ALU.add).then_inc(total_ready, 1)

        @block.tensor
        def _(pe):
            pe.wait_ge(consts, 2)

            def turn(i, k):
                pe.wait_ge(gathered[k], i * 16 + 16)
                wait_from(pe, xT_ready, i * U + (k - 1))
                for c in range(C):
                    last = pe.transpose(t_ps[k % 2][:, c], xg[:, k, c * P:(c + 1) * P], ident[:])
                last.then_inc(turned, 1)

            def gate_up(i, k):
                pe.wait_ge(w_loaded[k // 2], i * 48 + 48)
                pe.wait_ge(xT_ready, i * U + (k + 1))
                wait_from(pe, hid_ready, i * U + (k - 1))
                for n, w in enumerate((wg, wu)):
                    for c in range(C):
                        last = pe.matmul(gu_ps[k % 2][:, n], w[:, k, c], xT[:, k % 2, c], start=c == 0,
                                         stop=c == C - 1)
                last.then_inc(gu_ready, 1)

            def down(i, k):
                pe.wait_ge(hid_ready, i * U + (k + 1))
                wait_from(pe, yw_ready, i * U + (k - 1))
                pe.matmul(y_ps[k % 2][:], hid[:, k % 2], wd[:, k], start=True, stop=True).then_inc(y_ready, 1)

            turn(0, 0)
            turn(0, 1)
            gate_up(0, 0)

            def body(i, last):
                for k in range(U):
                    if not (last and k + 2 >= U):
                        turn(i + (k + 2) // U, (k + 2) % U)
                    if not (last and k + 1 >= U):
                        gate_up(i + (k + 1) // U, (k + 1) % U)
                    down(i, k)

            experts(pe, body)


def perceiver_layer(nc, d):
    B, S, D = d["x"].shape
    T = B * S
    experts, top, capacity = d["routerT"].shape[1], 8, P
    NH = d["Wq"].shape[1] // P
    KH = d["Wk"].shape[1] // P

    def scratch(name, shape):
        return nc.dram_tensor(f"scratch_{name}", shape, F32).ap()

    d = dict(d, experts=experts, top=top, capacity=capacity,
             qT=scratch("qT", (B, P, NH, S)), rq=scratch("rq", (P, B * NH * S // P)),
             rden=scratch("rden", (B * KH, NH // KH * S // P, P)), oT=scratch("oT", (B, P, NH, S)),
             tokens=scratch("tokens", (T + P, D)), slots=scratch("slots", (experts * capacity, 2)),
             sum0=scratch("sum0", (T + P, D)), sum1=scratch("sum1", (T + P, D)))
    query_stage(nc, d)
    attention_stage(nc, d)
    recurrent_stage(nc, dict(d, w_up=d["rnn_w_up"], w_gate=d["rnn_w_gate"], w_down=d["rnn_w_down"]))
    expert_stage(nc, dict(d, w_up=d["moe_w_up"], w_gate=d["moe_w_gate"], w_down=d["moe_w_down"]))


def kernel(**inputs):
    import numpy as np
    import concourse.bacc as bacc
    from concourse.bass_utils import run_bass_kernel_spmd

    given = {name: np.ascontiguousarray(a) for name, a in inputs.items()}
    context = given["ctx_2048"]
    B, K, D = context.shape
    ctxT = np.zeros((B, D // 128, 128, K + K % 2), context.dtype)
    ctxT[..., :K] = context.transpose(0, 2, 1).reshape(B, D // 128, 128, K)
    arrays = {
        "x": given["x"], "ctxT": ctxT,
        "Wq": given["L0_xattn_Wq"], "Wk": given["L0_xattn_Wk"], "Wv": given["L0_xattn_Wv"],
        "Wo": given["L0_xattn_Wo"],
        "q_norm_w": given["L0_xattn_q_norm_w"], "k_norm_w": given["L0_xattn_k_norm_w"],
        "w_f": given["L0_attn_w_f"], "w_i": given["L0_attn_w_i"], "w_v": given["L0_attn_w_v"],
        "w_q": given["L0_attn_w_q"], "w_ro": given["L0_attn_w_ro"],
        "rnn_w_up": given["L0_attn_w_up"], "rnn_w_gate": given["L0_attn_w_gate"],
        "rnn_w_down": given["L0_attn_w_down"], "init_state": given["L0_attn_init_state"],
        "routerT": np.ascontiguousarray(given["L0_ffn_gate_w"].T),
        "moe_w_gate": given["L0_ffn_w_gate"], "moe_w_up": given["L0_ffn_w_up"],
        "moe_w_down": given["L0_ffn_w_down"],
    }
    nc = bacc.Bacc("TRN2", target_bir_lowering=False, num_devices=1)
    d = {name: nc.dram_tensor(name, a.shape, mybir.dt.from_np(a.dtype), kind="ExternalInput").ap()
         for name, a in arrays.items()}
    d["keys"] = K
    d["out"] = nc.dram_tensor("out", given["x"].shape, F32, kind="ExternalOutput").ap()
    perceiver_layer(nc, d)
    r = run_bass_kernel_spmd(nc, [arrays], core_ids=[0])
    return r.results[0]["out"]
```

```python
import itertools
from contextlib import ExitStack

import concourse.bass as bass
from concourse import mybir

F32 = mybir.dt.float32
F32R = mybir.dt.float32r
ACT = mybir.ActivationFunctionType
ALU = mybir.AluOpType
AX_X = mybir.AxisListType.X
P = 128

LN_EPS = 1e-5
RMS_EPS = 1e-6
LOWEST = -3.0e38


def wait_from(eng, sem, count):
    if not isinstance(count, int) or count > 0:
        eng.wait_ge(sem, count)


def waits_here(eng, passed):
    eng.sem_inc(passed, 1)


def bounds(total, size):
    return [(i, min(i + size, total)) for i in range(0, total, size)]


class Memory:

    def __init__(self, nc, ctx, stage):
        self.nc, self.ctx, self.stage = nc, ctx, stage

    def sbuf(self, name, shape, dtype=F32):
        return self.ctx.enter_context(self.nc.sbuf_tensor(f"{self.stage}_{name}", shape, dtype))

    def psum(self, name, shape, dtype=F32):
        return self.ctx.enter_context(self.nc.psum_tensor(f"{self.stage}_{name}", shape, dtype))

    def sem(self, name):
        return self.ctx.enter_context(self.nc.semaphore(f"{self.stage}_{name}"))


def query_stage(nc, d):
    B, S, D = d["x"].shape
    T = B * S
    NT = T // P
    GT = min(512, T)
    NG = T // GT
    GB = GT // S
    C = D // P
    NH = d["Wq"].shape[1] // P
    HQ = 4
    BAT = NH // HQ
    PAIRS = NH * S // P
    TPG = GT // P
    RING = 4
    LAG = 3

    with ExitStack() as ctx:
        m = Memory(nc, ctx, "query")
        x_sb = m.sbuf("x", [P, NT, D])
        stats = m.sbuf("stats", [P, NT, 6])
        mv = m.sbuf("mv", [P, NT, 2])
        var = m.sbuf("var", [P, NT])
        rstd = m.sbuf("rstd", [P, NT])
        neg_half = m.sbuf("neg_half", [P, max(NT, GB * PAIRS)])
        ident = m.sbuf("ident", [P, P])
        xn = m.sbuf("xn", [P, NT, D])
        xT_hi = m.sbuf("xT_hi", [P, C, T], F32R)
        xT_lo = m.sbuf("xT_lo", [P, C, T], F32R)
        w_raw = m.sbuf("w_raw", [P, C, NH * P])
        w_hi = m.sbuf("w_hi", [P, C, NH * P], F32R)
        w_lo = m.sbuf("w_lo", [P, C, NH * P], F32R)
        norm_w = m.sbuf("norm_w", [P, 2])
        wqk = m.sbuf("wqk", [P, 1])
        head_ones = m.sbuf("head_ones", [P, NH, NH])
        select = m.sbuf("select", [P, NH, NH], F32R)
        qw = m.sbuf("qw", [P, 2, GB, HQ, S])
        sq = m.sbuf("sq", [P, RING, GT])
        sq_hi = m.sbuf("sq_hi", [P, RING, GT], F32R)
        sq_lo = m.sbuf("sq_lo", [P, RING, GT], F32R)
        mean_sq = m.sbuf("mean_sq", [NH, GB, 2, S])
        msq = m.sbuf("msq", [P, B, PAIRS])
        rq = m.sbuf("rq", [P, B, PAIRS])
        tp = [m.psum(f"tp{i}", [P, GT]) for i in range(2)]
        qp = [m.psum(f"qp{i}", [P, GT]) for i in range(RING)]
        ssq = m.psum("ssq", [NH, GT])
        turned_sq = m.psum("turned_sq", [P, GB, NH])

        x_loaded = [m.sem(f"x_loaded{g}") for g in range(NG)]
        w_loaded = m.sem("w_loaded")
        w_split_hi = m.sem("w_split_hi")
        w_split_lo = m.sem("w_split_lo")
        const_ready = m.sem("const_ready")
        stats_ready = m.sem("stats_ready")
        mean_ready = m.sem("mean_ready")
        var_ready = m.sem("var_ready")
        rstd_ready = m.sem("rstd_ready")
        xn_ready = m.sem("xn_ready")
        tp_ready = m.sem("tp_ready")
        hi_ready = m.sem("hi_ready")
        lo_ready = m.sem("lo_ready")
        wqk_ready = m.sem("wqk_ready")
        q_ready = m.sem("q_ready")
        sq_ready = m.sem("sq_ready")
        sq_hi_ready = m.sem("sq_hi_ready")
        sq_lo_ready = m.sem("sq_lo_ready")
        sq_summed = m.sem("sq_summed")
        mean_sq_ready = m.sem("mean_sq_ready")
        sq_turned = m.sem("sq_turned")
        qw_ready = m.sem("qw_ready")
        qw_stored = [m.sem(f"qw_stored{i}") for i in range(2)]
        msq_ready = m.sem("msq_ready")
        rq_ready = m.sem("rq_ready")
        rq_stored = m.sem("rq_stored")
        passed = m.sem("passed")
        block = ctx.enter_context(nc.Block())
        XB = NG * C

        @block.sync
        def _(sp):
            for g in range(NG):
                sp.dma_start(x_sb[:, g * TPG:(g + 1) * TPG], d["x"].rearrange("b s d -> (b s) d")[
                    g * GT:(g + 1) * GT].rearrange("(n p) d -> p n d", p=P)).then_inc(x_loaded[g], 16)
            sp.dma_start(w_raw[:], d["Wq"].rearrange("(c p) n -> p c n", p=P)).then_inc(w_loaded, 16)
            sp.dma_start(norm_w[:, 0:1], d["q_norm_w"].rearrange("(p a) -> p a", a=1)).then_inc(w_loaded, 16)
            sp.dma_start(norm_w[:, 1:2], d["k_norm_w"].rearrange("(p a) -> p a", a=1)).then_inc(w_loaded, 16)

            def group(g):
                for k in range(BAT):
                    sp.wait_ge(qw_ready, g * NH + (k + 1) * HQ)
                    waits_here(sp, passed)
                    sp.dma_start(
                        d["qT"][bass.ds(g * GB, GB), :, k * HQ:(k + 1) * HQ, :].rearrange("b p h s -> p b (h s)"),
                        qw[:, k % 2].rearrange("p b h s -> p b (h s)")).then_inc(qw_stored[k % 2], 16)

            with sp.Fori(0, NG) as g:
                group(g)
            sp.wait_ge(rq_ready, NG)
            sp.dma_start(d["rq"], rq[:].rearrange("p b j -> p (b j)")).then_inc(rq_stored, 16)
            for stored in qw_stored:
                sp.wait_ge(stored, 8 * NG * BAT)
            sp.wait_ge(rq_stored, 16)

        @block.gpsimd
        def _(pool):
            pool.memset(ident[:], 0.0).then_inc(const_ready, 1)
            pool.memset(head_ones[:], 0.0).then_inc(const_ready, 1)
            pool.memset(neg_half[:], -0.5).then_inc(const_ready, 1)
            pool.wait_ge(const_ready, 3)
            pool.affine_select(out=ident[:], in_=ident[:], compare_op=ALU.not_equal, fill=1.0, base=0,
                               pattern=[[-1, P]], channel_multiplier=1).then_inc(const_ready, 1)
            pool.memset(head_ones[:].rearrange("p a b -> p (a b)")[:, 0:NH * NH:NH + 1], 1.0).then_inc(const_ready, 1)
            for g in range(NG):
                tiles = slice(g * TPG, (g + 1) * TPG)
                pool.wait_ge(var_ready, g + 1)
                pool.tensor_tensor(rstd[:, tiles], var[:, tiles], neg_half[:, 0:TPG], ALU.pow).then_inc(rstd_ready, 1)
            exponent = neg_half[:, 0:GB * PAIRS].rearrange("p (b j) -> p b j", j=PAIRS)
            with pool.Fori(0, NG) as g:
                pool.wait_ge(msq_ready, g * 2 + 2)
                rows = bass.ds(g * GB, GB)
                pool.tensor_tensor(rq[:, rows], msq[:, rows], exponent, ALU.pow).then_inc(rq_ready, 1)

        @block.vector
        def _(dve):
            def normalize(g):
                dve.wait_ge(rstd_ready, g + 1)
                for t in range(g * TPG, (g + 1) * TPG):
                    dve.tensor_scalar(xn[:, t], x_sb[:, t], mv[:, t, 0:1], rstd[:, t:t + 1],
                                      ALU.subtract, ALU.mult).then_inc(xn_ready, 1)

            for g in range(NG):
                dve.wait_ge(x_loaded[g], 16)
                for t in range(g * TPG, (g + 1) * TPG):
                    dve.bn_stats(stats[:, t], x_sb[:, t]).then_inc(stats_ready, 1)
                for t in range(g * TPG, (g + 1) * TPG):
                    dve.wait_ge(stats_ready, t + 1)
                    dve.bn_aggr(mv[:, t], stats[:, t]).then_inc(mean_ready, 1)
                dve.wait_ge(mean_ready, (g + 1) * TPG)
                dve.tensor_scalar(var[:, g * TPG:(g + 1) * TPG], mv[:, g * TPG:(g + 1) * TPG, 1], LN_EPS, None,
                                  ALU.add).then_inc(var_ready, 1)
                if g > 0:
                    normalize(g - 1)
            normalize(NG - 1)
            dve.wait_ge(w_loaded, 48)
            dve.tensor_tensor(wqk[:], norm_w[:, 0:1], norm_w[:, 1:2], ALU.mult).then_inc(wqk_ready, 1)
            for c in range(C):
                dve.wait_ge(w_split_hi, c + 1)
                dve.tensor_tensor(w_lo[:, c], w_raw[:, c], w_hi[:, c], ALU.subtract).then_inc(w_split_lo, 1)
            for n in range(XB):
                g, c = n // C, n % C
                dve.wait_ge(hi_ready, n + 1)
                dve.tensor_tensor(xT_lo[:, c, g * GT:(g + 1) * GT], tp[n % 2][:],
                                  xT_hi[:, c, g * GT:(g + 1) * GT], ALU.subtract).then_inc(lo_ready, 1)
            dve.wait_ge(wqk_ready, 1)

            dve.wait_ge(const_ready, 5)
            dve.tensor_copy(select[:], head_ones[:]).then_inc(const_ready, 1)

            def mean_squares(g):
                dve.wait_ge(sq_summed, g * NH + NH)
                wait_from(dve, sq_turned, g)
                dve.tensor_scalar(mean_sq[:], ssq[:].rearrange("h (b s) -> h b s", s=S).unsqueeze(2).broadcast_to(
                    [NH, GB, 2, S]), 1.0 / P, RMS_EPS, ALU.mult, ALU.add).then_inc(mean_sq_ready, 1)

            def to_rows(g):
                dve.wait_ge(sq_turned, g + 1)
                for i in range(2):
                    rows = slice(i * S, (i + 1) * S)
                    dve.tensor_copy(msq[rows, bass.ds(g * GB, GB)], turned_sq[rows, :, i::2]).then_inc(msq_ready, 1)

            def group(g, first):
                for h in range(NH):
                    k, i = h // HQ, h % HQ
                    if not first and h == LAG:
                        mean_squares(g - 1)
                    if not first and h == 2 * LAG:
                        to_rows(g - 1)
                    dve.wait_ge(sq_ready, g * NH + (h + 1))
                    if i == 0 and not (first and k < 2):
                        dve.wait_ge(qw_stored[k % 2], g * (8 * BAT) + 16 * (k // 2))
                    dve.tensor_scalar(qw[:, k % 2, :, i], qp[h % RING][:].rearrange("p (b s) -> p b s", s=S),
                                      wqk[:, 0:1], None, ALU.mult).then_inc(qw_ready, 1)
                    dve.wait_ge(sq_hi_ready, g * NH + (h + 1))
                    wait_from(dve, sq_summed, g * NH + (h - RING + 1))
                    dve.tensor_tensor(sq_lo[:, h % RING], sq[:, h % RING], sq_hi[:, h % RING], ALU.subtract
                                      ).then_inc(sq_lo_ready, 1)

            group(0, True)
            if NG > 1:
                with dve.Fori(1, NG) as g:
                    group(g, False)
            mean_squares(NG - 1)
            to_rows(NG - 1)

        @block.scalar
        def _(act):
            act.wait_ge(w_loaded, 48)
            for c in range(C):
                act.activation(w_hi[:, c], w_raw[:, c], ACT.Copy).then_inc(w_split_hi, 1)
            for n in range(XB):
                g, c = n // C, n % C
                act.wait_ge(tp_ready, n + 1)
                act.activation(xT_hi[:, c, g * GT:(g + 1) * GT], tp[n % 2][:], ACT.Copy).then_inc(hi_ready, 1)

            def group(g, first):
                for h in range(NH):
                    act.wait_ge(q_ready, g * NH + (h + 1))
                    wait_from(act, sq_lo_ready, g * NH + (h - RING + 1))
                    act.activation(sq[:, h % RING], qp[h % RING][:], ACT.Square).then_inc(sq_ready, 1)
                    act.wait_ge(sq_ready, g * NH + (h + 1))
                    wait_from(act, sq_summed, g * NH + (h - RING + 1))
                    act.activation(sq_hi[:, h % RING], sq[:, h % RING], ACT.Copy).then_inc(sq_hi_ready, 1)

            group(0, True)
            if NG > 1:
                with act.Fori(1, NG) as g:
                    group(g, False)

        @block.tensor
        def _(pe):
            pe.wait_ge(const_ready, 5)
            for n in range(XB):
                g, c = n // C, n % C
                pe.wait_ge(xn_ready, (g + 1) * TPG)
                if n >= 2:
                    pe.wait_ge(lo_ready, n - 1)
                for t in range(TPG):
                    last = pe.transpose(tp[n % 2][:, t * P:(t + 1) * P], xn[:, g * TPG + t, c * P:(c + 1) * P],
                                        ident[:])
                last.then_inc(tp_ready, 1)
            pe.wait_ge(lo_ready, XB)
            pe.wait_ge(w_split_lo, C)
            pe.wait_ge(const_ready, 6)

            def sum_squares(g, h):
                pe.wait_ge(sq_lo_ready, g * NH + (h + 1))
                if h == 0:
                    wait_from(pe, mean_sq_ready, g)
                for n, part in enumerate((sq_hi, sq_lo)):
                    last = pe.matmul(ssq[:], select[:, h], part[:, h % RING], start=h == 0 and n == 0,
                                     stop=h == NH - 1 and n == 1, skip_group_check=True)
                last.then_inc(sq_summed, 1)

            def turn_squares(g):
                pe.wait_ge(mean_sq_ready, g + 1)
                wait_from(pe, msq_ready, g * 2)
                waits_here(pe, passed)
                for b in range(GB):
                    last = pe.transpose(turned_sq[:, b], mean_sq[:, b].rearrange("h a s -> h (a s)"),
                                        ident[:NH, :NH])
                last.then_inc(sq_turned, 1)

            def group(g, first):
                for h in range(NH):
                    wait_from(pe, qw_ready, g * NH + (h - RING + 1))
                    tok = bass.ds(g * GT, GT)
                    n = 0
                    for w, xs in ((w_hi, xT_hi), (w_hi, xT_lo), (w_lo, xT_hi)):
                        for c in range(C):
                            last = pe.matmul(qp[h % RING][:], w[:, c, h * P:(h + 1) * P], xs[:, c, tok],
                                             start=n == 0, stop=n == 3 * C - 1)
                            n += 1
                    last.then_inc(q_ready, 1)
                    if h >= LAG:
                        sum_squares(g, h - LAG)
                    elif not first:
                        sum_squares(g - 1, NH + h - LAG)
                    if not first and h == 2 * LAG - 1:
                        turn_squares(g - 1)

            group(0, True)
            if NG > 1:
                with pe.Fori(1, NG) as g:
                    group(g, False)
            for h in range(NH - LAG, NH):
                sum_squares(NG - 1, h)
            turn_squares(NG - 1)


def attention_stage(nc, d):
    B, S, D = d["x"].shape
    KEYS = d["keys"]
    C = D // P
    KH = d["Wk"].shape[1] // P
    NH = d["Wq"].shape[1] // P
    QPK = NH // KH
    ROWS = QPK * S
    QT = ROWS // P
    PAIRS = NH * S // P
    PADDED = d["ctxT"].shape[3]
    TILES = bounds(PADDED, P)
    NT = len(TILES)
    SLOTS = [list(range(i, min(i + 2, NT))) for i in range(0, NT, 2)]
    NS = len(SLOTS)
    GROUPS = [list(range(i, min(i + 4, NT))) for i in range(0, NT, 4)]
    NGR = len(GROUPS)
    NC = 4
    piece = (PADDED // NC) // 2 * 2
    ends = [PADDED - piece * (NC - 1 - i) for i in range(NC)]
    CHUNKS = list(zip([0] + ends[:-1], ends))
    NSC = QT * NC
    SCORES = {0: [(0, 0), (1, 0)], 1: [(0, 1), (1, 1)], 2: [(0, 2), (0, 3)], 3: [(1, 2), (1, 3)]}
    COMPLETE = {2: 0, 3: 1}
    HALVES = bounds(KEYS, KEYS // 2 + 1)
    EXPS = {3: (0, 0), 4: (1, 0), 5: (0, 1), 6: (1, 1)}
    NE = len(EXPS)
    TURNED = {0: (0, 1), 1: (0, 2), 2: (0, 3), 5: (1, 0)}
    ORDER = [c for s in sorted(SCORES) for c in SCORES[s]]
    assert NS == 7 and NGR == 4 and QT == 2 and KH == 4

    def at(b, h, off, per, more):
        return b * (KH * per) + ((h + off) * per + more)

    def moved(b, h, off):
        return b * (KH // 2 * 16) + ((h + off) // 2 * 16 + 16)

    with ExitStack() as ctx:
        m = Memory(nc, ctx, "attn")
        c_raw = m.sbuf("c_raw", [P, C, PADDED])
        c_hi = m.sbuf("c_hi", [P, C, PADDED], F32R)
        c_lo = m.sbuf("c_lo", [P, C, PADDED], F32R)
        w_raw = m.sbuf("w_raw", [P, C, KH, 2, P])
        w_hi = m.sbuf("w_hi", [P, C, KH, 2 * P], F32R)
        w_lo = m.sbuf("w_lo", [P, C, KH, 2 * P], F32R)
        k_raw = m.sbuf("k_raw", [P, NT, P])
        k_sq = m.sbuf("k_sq", [P, 4, P])
        k_ss = m.sbuf("k_ss", [P, NT])
        k_ms = m.sbuf("k_ms", [P, NT])
        k_r = m.sbuf("k_r", [P, NT])
        k_unit = m.sbuf("k_unit", [P, 2, 4, P])
        kT_hi = m.sbuf("kT_hi", [P, 2, NT * P], F32R)
        kT_lo = m.sbuf("kT_lo", [P, 2, NT * P], F32R)
        v_hi = m.sbuf("v_hi", [P, 2, NT, P], F32R)
        v_lo = m.sbuf("v_lo", [P, 2, NT, P], F32R)
        q_raw = m.sbuf("q_raw", [P, KH, ROWS])
        q_hi = m.sbuf("q_hi", [P, KH, ROWS], F32R)
        q_lo = m.sbuf("q_lo", [P, KH, ROWS], F32R)
        rq = m.sbuf("rq", [P, B * PAIRS])
        rqb = m.sbuf("rqb", [P, PAIRS])
        probs = m.sbuf("probs", [P, 2, QT, KEYS])
        pT = m.sbuf("pT", [P, 2, 2, 2, ROWS], F32R)
        piece_max = m.sbuf("piece_max", [P, QT, NC])
        row_max = m.sbuf("row_max", [P, QT])
        shift = m.sbuf("shift", [P, QT])
        den_parts = m.sbuf("den_parts", [P, 2, QT, 2])
        den = m.sbuf("den", [P, 2, QT])
        rden = m.sbuf("rden", [P, 2, QT])
        rden_b = m.sbuf("rden_b", [P, 2, ROWS])
        oT = m.sbuf("oT", [P, 2, ROWS])
        ident = m.sbuf("ident", [P, P])
        neg_half = m.sbuf("neg_half", [P, 4])
        eps = m.sbuf("eps", [P, 4])
        s_ps = [m.psum(f"s{i}", [P, 512]) for i in range(2)]
        kv_ps = [m.psum(f"kv{i}", [P, 2, 2 * P]) for i in range(2)]
        pT_ps = [m.psum(f"pT{i}", [P, 2, ROWS]) for i in range(2)]
        kT_ps = m.psum("kT_ps", [P, 4 * P])
        o_ps = m.psum("o_ps", [P, ROWS])

        consts = m.sem("consts")
        w_loaded = m.sem("w_loaded")
        w_hi_ready = m.sem("w_hi_ready")
        w_lo_ready = m.sem("w_lo_ready")
        c_loaded = m.sem("c_loaded")
        c_hi_ready = m.sem("c_hi_ready")
        c_lo_ready = m.sem("c_lo_ready")
        q_loaded = m.sem("q_loaded")
        q_hi_ready = m.sem("q_hi_ready")
        q_lo_ready = m.sem("q_lo_ready")
        rqb_ready = m.sem("rqb_ready")
        kv_ready = m.sem("kv_ready")
        v_hi_ready = m.sem("v_hi_ready")
        k_copied = m.sem("k_copied")
        v_lo_ready = m.sem("v_lo_ready")
        k_squared = m.sem("k_squared")
        k_summed = m.sem("k_summed")
        k_mean = m.sem("k_mean")
        k_r_ready = m.sem("k_r_ready")
        k_unit_ready = m.sem("k_unit_ready")
        kT_ready = m.sem("kT_ready")
        kT_hi_ready = m.sem("kT_hi_ready")
        kT_lo_ready = m.sem("kT_lo_ready")
        s_ready = m.sem("s_ready")
        s_copied = m.sem("s_copied")
        max_ready = m.sem("max_ready")
        shift_ready = m.sem("shift_ready")
        exp_ready = m.sem("exp_ready")
        den_ready = m.sem("den_ready")
        rden_ready = m.sem("rden_ready")
        rden_stored = m.sem("rden_stored")
        rden_b_ready = [m.sem(f"rden_b_ready{i}") for i in range(2)]
        pT_ready = m.sem("pT_ready")
        pT_hi_ready = m.sem("pT_hi_ready")
        pT_lo_ready = m.sem("pT_lo_ready")
        pv_done = m.sem("pv_done")
        o_ready = m.sem("o_ready")
        o_stored = [m.sem(f"o_stored{i}") for i in range(2)]
        passed = m.sem("passed")
        block = ctx.enter_context(nc.Block())

        def pipeline(eng, step):
            step(-1, KH - 1, False, False, True)
            step(0, 0, True, False, True)
            for h in range(1, KH):
                step(0, h, True, True, h < KH - 1 or B > 1)
            if B > 2:
                with eng.Fori(1, B - 1) as b:
                    for h in range(KH):
                        step(b, h, True, True, True)
            if B > 1:
                for h in range(KH):
                    step(B - 1, h, True, True, h < KH - 1)
            step(B, 0, False, True, False)

        def j_bank(b, h, j):
            return ((h + 1) % 2 * NS + j) % 2

        def turned(b, h, j):
            off, i = (-1, j + 1) if j + 1 < NS else (0, 0)
            return off, i, ((h + off) % 2 * NS + i) % 2

        def s_bank(h, n):
            return s_ps[n % 2]

        def keys_of(tile):
            return min(TILES[tile][1], KEYS) - TILES[tile][0]

        def width(tiles):
            return TILES[tiles[-1]][1] - TILES[tiles[0]][0]

        def queries_after(b, h, scores, split):
            if scores and h == 0 and not (isinstance(b, int) and b == 0):
                split(b, KH - 1)
            if scores and h > 0 and not (isinstance(b, int) and b == B - 1):
                split(b + 1, h - 1)

        @block.sync
        def _(sp):
            for c in range(C):
                for n, w in enumerate((d["Wk"], d["Wv"])):
                    sp.dma_start(w_raw[:, c, :, n], w[c * P:(c + 1) * P, :].rearrange("p (h e) -> p h e", e=P)
                                 ).then_inc(w_loaded, 16)
            sp.dma_start(rq[:], d["rq"]).then_inc(w_loaded, 16)

            def load_context(b):
                wait_from(sp, c_hi_ready, b * NS)
                wait_from(sp, c_lo_ready, b * NS)
                waits_here(sp, passed)
                sp.dma_start(c_raw[:], d["ctxT"][bass.ds(b, 1)].rearrange("a c p k -> (a p) c k")
                             ).then_inc(c_loaded, 16)

            def load_queries(b):
                wait_from(sp, q_lo_ready, b * KH)
                waits_here(sp, passed)
                sp.dma_start(q_raw[:].rearrange("p h r -> p (h r)"),
                             d["qT"][bass.ds(b, 1)].rearrange("a p h s -> (a p) (h s)")).then_inc(q_loaded, 16)

            load_context(0)
            load_queries(0)

            def step(b, h, scores, values, project):
                if scores and not (isinstance(b, int) and b == B - 1):
                    if h == 0:
                        load_context(b + 1)
                    if h == 1:
                        load_queries(b + 1)
                if scores:
                    sp.wait_ge(rden_ready, at(b, h, 0, 1, 1))
                    waits_here(sp, passed)
                    with nc.allow_non_contiguous_dma("256 numbers, a column each of two"):
                        sp.dma_start(d["rden"][bass.ds(b * KH + h, 1)].rearrange("u q p -> p (u q)"),
                                     rden[:, h % 2]).then_inc(rden_stored, 16)
                    sp.wait_ge(rden_stored, at(b, h, 0, 16, 16))
                    waits_here(sp, passed)
                    wait_from(sp, o_ready, at(b, h, 0, 1, -1))
                    waits_here(sp, passed)
                    sp.dma_start(rden_b[:, h % 2], d["rden"][bass.ds(b * KH + h, 1)].rearrange(
                        "u q p -> u (q p)").broadcast_to([P, ROWS])).then_inc(rden_b_ready[h % 2], 16)
                if values:
                    store_output(b, h)

            def store_output(b, h):
                hh = (h - 1) % KH
                bb = b if h > 0 else b - 1
                sp.wait_ge(o_ready, at(b, h, -1, 1, 1))
                waits_here(sp, passed)
                sp.dma_start(d["oT"][bass.ds(bb, 1), :, hh * QPK:(hh + 1) * QPK, :].rearrange(
                    "a p h s -> (a p) (h s)"), oT[:, hh % 2]).then_inc(o_stored[hh % 2], 16)

            pipeline(sp, step)
            for stored in o_stored:
                sp.wait_ge(stored, 8 * KH * B)

        @block.gpsimd
        def _(pool):
            pool.memset(ident[:], 0.0).then_inc(consts, 1)
            pool.memset(neg_half[:], -0.5).then_inc(consts, 1)
            pool.memset(eps[:], P * RMS_EPS).then_inc(consts, 1)
            pool.wait_ge(consts, 3)
            pool.affine_select(out=ident[:], in_=ident[:], compare_op=ALU.not_equal, fill=1.0, base=0,
                               pattern=[[-1, P]], channel_multiplier=1).then_inc(consts, 1)
            pool.wait_ge(consts, 4)

            def norms(b, h, g):
                tiles = GROUPS[g]
                n, rows = len(tiles), width(tiles[:1])
                sl = slice(tiles[0], tiles[-1] + 1)
                pool.wait_ge(k_copied, at(b, h, 1, NS, tiles[-1] // 2 + 1))
                wait_from(pool, k_summed, at(b, h, 1, NGR, g))
                pool.tensor_tensor(k_sq[:rows, 0:n], k_raw[:rows, sl], k_raw[:rows, sl], ALU.mult
                                   ).then_inc(k_squared, 1)
                pool.wait_ge(k_summed, at(b, h, 1, NGR, g + 1))
                pool.tensor_tensor(k_ms[:rows, sl], k_ss[:rows, sl], eps[:rows, 0:n], ALU.add
                                   ).then_inc(k_mean, 1)
                pool.wait_ge(k_mean, at(b, h, 1, NGR, g + 1))
                wait_from(pool, k_unit_ready, at(b, h, 0, NGR, g + 1))
                pool.tensor_tensor(k_r[:rows, sl], k_ms[:rows, sl], neg_half[:rows, 0:n], ALU.pow
                                   ).then_inc(k_r_ready, 1)
                pool.wait_ge(k_r_ready, at(b, h, 1, NGR, g + 1))
                wait_from(pool, kT_ready, at(b, h, 1, NGR, g - 1))
                pool.tensor_tensor(k_unit[:rows, g % 2, 0:n], k_raw[:rows, sl],
                                   k_r[:rows, sl].unsqueeze(2).broadcast_to([rows, n, P]), ALU.mult
                                   ).then_inc(k_unit_ready, 1)

            def split_queries(b, h):
                pool.wait_ge(q_hi_ready, at(b, h, 0, 1, 1))
                pool.tensor_tensor(q_lo[:, h], q_raw[:, h], q_hi[:, h], ALU.subtract).then_inc(q_lo_ready, 1)

            def step(b, h, scores, values, project):
                if isinstance(b, int) and b < 0:
                    for hh in range(KH):
                        split_queries(0, hh)
                for j in range(NS):
                    if project:
                        if j in (2, 4, 6):
                            norms(b, h, (j - 2) // 2)
                if project:
                    norms(b, h, 3)
                queries_after(b, h, scores, split_queries)

            pipeline(pool, step)

        @block.scalar
        def _(act):
            act.wait_ge(w_loaded, 16 * (2 * C + 1))
            for c in range(C):
                act.activation(w_hi[:, c], w_raw[:, c].rearrange("p h n e -> p h (n e)"), ACT.Copy
                               ).then_inc(w_hi_ready, 1)

            def split_context(b, j):
                a, z = TILES[SLOTS[j][0]][0], TILES[SLOTS[j][-1]][1]
                act.wait_ge(c_loaded, b * 16 + 16)
                wait_from(act, kv_ready, at(b, 0, -1, NS, NS + j + 1) - NS)
                act.activation(c_hi[:, :, a:z], c_raw[:, :, a:z], ACT.Copy).then_inc(c_hi_ready, 1)

            def split_queries(b, h):
                act.wait_ge(q_loaded, b * 16 + 16)
                wait_from(act, s_ready, at(b, h, -KH + 1, NSC, 0))
                act.activation(q_hi[:, h], q_raw[:, h], ACT.Copy).then_inc(q_hi_ready, 1)

            def exponentials(b, h, q, half):
                a, z = HALVES[half]
                act.wait_ge(shift_ready, at(b, h, 0, QT, q + 1))
                act.activation(probs[:, h % 2, q, a:z], probs[:, h % 2, q, a:z], ACT.Exp, bias=shift[:, q:q + 1],
                               scale=rqb[:, h * QT + q:h * QT + q + 1],
                               accum_out=den_parts[:, h % 2, q, half:half + 1]).then_inc(exp_ready, 1)

            def step(b, h, scores, values, project):
                first = isinstance(b, int) and b < 0
                if first:
                    for j in range(NS):
                        split_context(0, j)
                    for hh in range(KH):
                        split_queries(0, hh)
                for j in range(NS):
                    if scores if j == NS - 1 else values:
                        off, i, bank = turned(b, h, j)
                        n = len(SLOTS[i])
                        rows = keys_of(SLOTS[i][0])
                        act.wait_ge(pT_ready, at(b, h, off, NS, i + 1))
                        wait_from(act, pv_done, at(b, h, off, NS, i - 1))
                        act.activation(pT[:rows, bank, 0:n, 0], pT_ps[bank][:rows, 0:n], ACT.Copy
                                       ).then_inc(pT_hi_ready, 1)
                    if scores and j in EXPS:
                        exponentials(b, h, *EXPS[j])
                    if j in TURNED and (scores if TURNED[j][0] == 0 else project):
                        off, g = TURNED[j]
                        w = width(GROUPS[g])
                        a = TILES[GROUPS[g][0]][0]
                        act.wait_ge(kT_ready, at(b, h, off, NGR, g + 1))
                        wait_from(act, s_ready, at(b, h, off - 1, NSC, 0))
                        act.activation(kT_hi[:, (h + off) % 2, a:a + w], kT_ps[:, 0:w], ACT.Copy
                                       ).then_inc(kT_hi_ready, 1)
                    if project:
                        n = len(SLOTS[j])
                        rows = width(SLOTS[j][:1])
                        sl = slice(SLOTS[j][0], SLOTS[j][-1] + 1)
                        act.wait_ge(kv_ready, at(b, h, 1, NS, j + 1))
                        wait_from(act, pv_done, at(b, h, -1, NS, j + 1))
                        act.activation(v_hi[:rows, (h + 1) % 2, sl], kv_ps[j_bank(b, h, j)][:rows, 0:n, P:2 * P],
                                       ACT.Copy).then_inc(v_hi_ready, 1)
                        wait_from(act, k_unit_ready, at(b, h, 0, NGR, SLOTS[j][-1] // 4 + 1))
                        act.activation(k_raw[:rows, sl], kv_ps[j_bank(b, h, j)][:rows, 0:n, 0:P], ACT.Copy
                                       ).then_inc(k_copied, 1)
                    if project and h == KH - 2 and not (isinstance(b, int) and b == B - 1) and not first:
                        split_context(b + 1, j)
                queries_after(b, h, scores, split_queries)

            pipeline(act, step)

        @block.vector
        def _(dve):
            for c in range(C):
                dve.wait_ge(w_hi_ready, c + 1)
                dve.tensor_tensor(w_lo[:, c], w_raw[:, c].rearrange("p h n e -> p h (n e)"), w_hi[:, c],
                                  ALU.subtract).then_inc(w_lo_ready, 1)
            dve.wait_ge(w_loaded, 16 * (2 * C + 1))

            def split_context(b, j):
                a, z = TILES[SLOTS[j][0]][0], TILES[SLOTS[j][-1]][1]
                dve.wait_ge(c_hi_ready, b * NS + (j + 1))
                dve.tensor_tensor(c_lo[:, :, a:z], c_raw[:, :, a:z], c_hi[:, :, a:z], ALU.subtract
                                  ).then_inc(c_lo_ready, 1)

            def sum_squares(b, h, off, g):
                tiles = GROUPS[g]
                n, rows = len(tiles), width(tiles[:1])
                sl = slice(tiles[0], tiles[-1] + 1)
                dve.wait_ge(k_squared, at(b, h, off, NGR, g + 1))
                wait_from(dve, k_mean, at(b, h, off - 1, NGR, g + 1))
                dve.tensor_reduce(k_ss[:rows, sl], k_sq[:rows, 0:n], AX_X, ALU.add).then_inc(k_summed, 1)

            def denominators(b, h):
                par = (h - 1) % 2
                dve.wait_ge(exp_ready, at(b, h, -1, NE, NE))
                dve.tensor_tensor(den[:, par], den_parts[:, par, :, 0], den_parts[:, par, :, 1],
                                  ALU.add).then_inc(den_ready, 1)
                dve.wait_ge(den_ready, at(b, h, -1, 1, 1))
                wait_from(dve, rden_stored, at(b, h, -1, 16, -16))
                dve.reciprocal(rden[:, par], den[:, par]).then_inc(rden_ready, 1)

            def output(b, h):
                par = (h - 1) % 2
                dve.wait_ge(pv_done, at(b, h, -1, NS, NS))
                dve.wait_ge(rden_b_ready[par], moved(b, h, -1))
                wait_from(dve, o_stored[par], moved(b, h, -3))
                dve.tensor_tensor(oT[:, par], o_ps[:], rden_b[:, par], ALU.mult).then_inc(o_ready, 1)

            def copy_scores(b, h, q, c):
                n = ORDER.index((q, c))
                a, z = CHUNKS[c]
                z = min(z, KEYS)
                dve.wait_ge(s_ready, at(b, h, 0, NSC, n + 1))
                if n == 0:
                    wait_from(dve, pT_ready, at(b, h, -1, NS, 0))
                    wait_from(dve, max_ready, at(b, h, 0, QT, 0))
                dve.tensor_scalar(probs[:, h % 2, q, a:z], s_bank(h, n)[:, 0:z - a], 1.0, LOWEST,
                                  ALU.mult, ALU.max, accum_out=piece_max[:, q, c:c + 1]
                                  ).then_inc(s_copied, 1)

            def step(b, h, scores, values, project):
                first = isinstance(b, int) and b < 0
                if first:
                    for j in range(NS):
                        split_context(0, j)
                for j in range(NS):
                    if scores and j == 0 and h == 0:
                        wait_from(dve, exp_ready, at(b, 0, 0, NE, 0))
                        dve.tensor_copy(rqb[:], rq[:, bass.ds(b * PAIRS, PAIRS)]).then_inc(rqb_ready, 1)
                    if scores if j == NS - 1 else values:
                        off, i, bank = turned(b, h, j)
                        n = len(SLOTS[i])
                        rows = keys_of(SLOTS[i][0])
                        dve.wait_ge(pT_hi_ready, at(b, h, off, NS, i + 1))
                        dve.tensor_tensor(pT[:rows, bank, 0:n, 1], pT_ps[bank][:rows, 0:n], pT[:rows, bank, 0:n, 0],
                                          ALU.subtract).then_inc(pT_lo_ready, 1)
                    if values and j == NS - 1:
                        output(b, h)
                    if scores and j in SCORES:
                        copy_scores(b, h, *SCORES[j][0])
                    if j in TURNED and (scores if TURNED[j][0] == 0 else project):
                        off, g = TURNED[j]
                        w = width(GROUPS[g])
                        a = TILES[GROUPS[g][0]][0]
                        par = (h + off) % 2
                        dve.wait_ge(kT_hi_ready, at(b, h, off, NGR, g + 1))
                        dve.tensor_tensor(kT_lo[:, par, a:a + w], kT_ps[:, 0:w], kT_hi[:, par, a:a + w],
                                          ALU.subtract).then_inc(kT_lo_ready, 1)
                    if project:
                        n = len(SLOTS[j])
                        rows = width(SLOTS[j][:1])
                        sl = slice(SLOTS[j][0], SLOTS[j][-1] + 1)
                        dve.wait_ge(k_copied, at(b, h, 1, NS, j + 1))
                        dve.tensor_tensor(v_lo[:rows, (h + 1) % 2, sl], kv_ps[j_bank(b, h, j)][:rows, 0:n, P:2 * P],
                                          v_hi[:rows, (h + 1) % 2, sl], ALU.subtract).then_inc(v_lo_ready, 1)
                    if scores and j in SCORES:
                        copy_scores(b, h, *SCORES[j][1])
                    if scores and j in COMPLETE:
                        q = COMPLETE[j]
                        dve.wait_ge(s_copied, at(b, h, 0, NSC, 1 + max(i for i, c in enumerate(ORDER) if c[0] == q)))
                        dve.wait_ge(rqb_ready, b + 1)
                        dve.tensor_reduce(row_max[:, q:q + 1], piece_max[:, q], AX_X, ALU.max).then_inc(max_ready, 1)
                        dve.wait_ge(max_ready, at(b, h, 0, QT, q + 1))
                        wait_from(dve, exp_ready, at(b, h, 0, NE, 0))
                        dve.tensor_scalar(shift[:, q:q + 1], row_max[:, q:q + 1],
                                          rqb[:, h * QT + q:h * QT + q + 1], -1.0, ALU.mult, ALU.mult
                                          ).then_inc(shift_ready, 1)
                    if project and h == KH - 2 and not (isinstance(b, int) and b == B - 1) and not first:
                        split_context(b + 1, j)
                    if values and j == 0:
                        denominators(b, h)
                    if scores and j == 0:
                        sum_squares(b, h, 0, 3)
                    if project and j in (2, 4, 6):
                        sum_squares(b, h, 1, (j - 2) // 2)

            pipeline(dve, step)

        @block.tensor
        def _(pe):
            pe.wait_ge(consts, 4)
            pe.wait_ge(w_lo_ready, C)

            def project_slot(b, h, j):
                hh = (h + 1) % KH
                bank = kv_ps[j_bank(b, h, j)]
                if hh == 0:
                    pe.wait_ge(c_lo_ready, (b + 1) * NS + (j + 1))
                wait_from(pe, v_lo_ready, at(b, h, 1, NS, j - 1))
                for i, t in enumerate(SLOTS[j]):
                    a, z = TILES[t]
                    n = 0
                    for cs, w in ((c_hi, w_hi), (c_hi, w_lo), (c_lo, w_hi)):
                        for c in range(C):
                            last = pe.matmul(bank[:z - a, i], cs[:, c, a:z], w[:, c, hh], start=n == 0,
                                             stop=n == 3 * C - 1)
                            n += 1
                last.then_inc(kv_ready, 1)

            def score_piece(b, h, q, c):
                n = ORDER.index((q, c))
                a, z = CHUNKS[c]
                groups = 1 + max(t for t in range(NT) if TILES[t][0] < z) // 4
                pe.wait_ge(kT_lo_ready, at(b, h, 0, NGR, groups))
                pe.wait_ge(q_lo_ready, at(b, h, 0, 1, 1))
                wait_from(pe, s_copied, at(b, h, 0, NSC, n - 1))
                for i, (x, y) in enumerate(((q_hi, kT_hi), (q_hi, kT_lo), (q_lo, kT_hi))):
                    last = pe.matmul(s_bank(h, n)[:, 0:z - a], x[:, h, q * P:(q + 1) * P], y[:, h % 2, a:z],
                                     start=i == 0, stop=i == 2)
                last.then_inc(s_ready, 1)

            def turn_keys(b, h, off, g):
                pe.wait_ge(k_unit_ready, at(b, h, off, NGR, g + 1))
                wait_from(pe, kT_lo_ready, at(b, h, off, NGR, g))
                for i, t in enumerate(GROUPS[g]):
                    a, z = TILES[t]
                    last = pe.transpose(kT_ps[:, i * P:i * P + z - a], k_unit[:z - a, g % 2, i], ident[:z - a, :z - a])
                last.then_inc(kT_ready, 1)

            def turn_probs(b, h, j):
                off, slot, bank = turned(b, h, j)
                behind = TILES[SLOTS[slot][-1]][1] > HALVES[0][1]
                pe.wait_ge(exp_ready, at(b, h, off, NE, NE if behind else NE // 2))
                wait_from(pe, pT_lo_ready, at(b, h, off, NS, slot - 1))
                par = (h + off) % 2
                for i, t in enumerate(SLOTS[slot]):
                    a = TILES[t][0]
                    n = keys_of(t)
                    for q in range(QT):
                        last = pe.transpose(pT_ps[bank][:n, i, q * P:(q + 1) * P], probs[:, par, q, a:a + n],
                                            ident[:])
                last.then_inc(pT_ready, 1)

            def add_values(b, h, j):
                par = (h - 1) % 2
                bank = (par * NS + j) % 2
                pe.wait_ge(pT_lo_ready, at(b, h, -1, NS, j + 1))
                pe.wait_ge(v_lo_ready, at(b, h, -1, NS, j + 1))
                if j == 0:
                    wait_from(pe, o_ready, at(b, h, -1, 1, 0))
                for i, t in enumerate(SLOTS[j]):
                    n = keys_of(t)
                    for n3, (v, low) in enumerate(((v_hi, 0), (v_hi, 1), (v_lo, 0))):
                        last = pe.matmul(o_ps[:], v[:n, par, t], pT[:n, bank, i, low], start=t == 0 and n3 == 0,
                                         stop=t == NT - 1 and n3 == 2)
                last.then_inc(pv_done, 1)

            def step(b, h, scores, values, project):
                for j in range(NS):
                    if scores if j == NS - 1 else values:
                        turn_probs(b, h, j)
                    if scores and j in SCORES:
                        score_piece(b, h, *SCORES[j][0])
                    if j in TURNED and (scores if TURNED[j][0] == 0 else project):
                        turn_keys(b, h, *TURNED[j])
                    if values:
                        add_values(b, h, j)
                    if project:
                        project_slot(b, h, j)
                    if scores and j in SCORES:
                        score_piece(b, h, *SCORES[j][1])

            pipeline(pe, step)


def recurrent_stage(nc, d):
    B, S, D = d["x"].shape
    T = B * S
    C = D // P
    NH = d["Wo"].shape[0] // P
    GT = min(512, T)
    GB = GT // S
    NG = T // GT
    NT = GT // P
    HT = NT // 2
    BT = P // S
    E = d["experts"]
    TOP = d["top"]
    CAP = d["capacity"]
    SLOTS = E * CAP
    N_IN = 6

    with ExitStack() as ctx:
        m = Memory(nc, ctx, "rec")
        wo_hi = m.sbuf("wo_hi", [P, NH, D], F32R)
        wo_lo = m.sbuf("wo_lo", [P, NH, D], F32R)
        w_in_hi = m.sbuf("w_in_hi", [P, N_IN, C, D], F32R)
        w_in_lo = m.sbuf("w_in_lo", [P, N_IN, C, D], F32R)
        w_ro = m.sbuf("w_ro", [P, C, D])
        w_down = m.sbuf("w_down", [P, C, D])
        init = m.sbuf("init", [P, C])
        router = m.sbuf("router", [P, C, E])
        oT = m.sbuf("oT", [P, 2, NH, BT, S])
        oT_hi = m.sbuf("oT_hi", [P, 2, NH, P], F32R)
        oT_lo = m.sbuf("oT_lo", [P, 2, NH, P], F32R)
        x = m.sbuf("x", [P, NT, D])
        x1 = m.sbuf("x1", [P, NT, D])
        x2 = m.sbuf("x2", [P, NT, D])
        xn = m.sbuf("xn", [P, NT, D])
        xT = m.sbuf("xT", [P, C, GT])
        xT_hi = m.sbuf("xT_hi", [P, C, GT], F32R)
        xT_lo = m.sbuf("xT_lo", [P, C, GT], F32R)
        stats = m.sbuf("stats", [P, NT, 6])
        mv = m.sbuf("mv", [P, NT, 2])
        var = m.sbuf("var", [P, NT])
        rstd = m.sbuf("rstd", [P, NT])
        neg_half = m.sbuf("neg_half", [P, NT])
        work = m.sbuf("work", [P, 7, C, GT])
        f, g_, sv, states, z, sz, mlp = (work[:, i] for i in range(7))
        flat = work[:].rearrange("p i c t -> p (i c t)")
        wo = flat[:, 0:NH * D].rearrange("p (h n) -> p h n", n=D)
        w_in = flat[:, NH * D:NH * D + N_IN * C * D].rearrange("p (w c n) -> p w c n", c=C, n=D)
        ident = m.sbuf("ident", [P, P])
        before = m.sbuf("before", [P, P])
        ones = m.sbuf("ones", [P, P])
        slot_base = m.sbuf("slot_base", [P, E])
        top_logit = m.sbuf("top_logit", [P, NT])
        expd = m.sbuf("expd", [P, NT, E])
        esum = m.sbuf("esum", [P, NT])
        resum = m.sbuf("resum", [P, NT])
        probs = m.sbuf("probs", [P, NT, E])
        top8 = m.sbuf("top8", [P, NT, 8])
        rest = m.sbuf("rest", [P, NT, E])
        chosen = m.sbuf("chosen", [P, NT, E])
        taken = m.sbuf("taken", [P, E])
        tmp = m.sbuf("tmp", [P, NT, E])
        kept = m.sbuf("kept", [P, NT, E])
        code = m.sbuf("code", [P, NT, E])
        code8 = m.sbuf("code8", [P, NT, TOP])
        same = m.sbuf("same", [P, NT, TOP, E])
        place = m.sbuf("place", [P, NT, TOP], mybir.dt.int32)
        pair = m.sbuf("pair", [P, NT, TOP, 2])
        token = m.sbuf("token", [P, NT])
        zero = m.sbuf("zero", [P, NT * D])
        empty = m.sbuf("empty", [P, E, 2])
        y_ps = [m.psum(f"y{i}", [P, 512]) for i in range(2)]
        in_ps = [m.psum(f"in{i}", [P, GT]) for i in range(3)]
        turn_ps = [m.psum("turn", [P, GT]), in_ps[2]]
        assert C == 2
        l_ps = m.psum("l", [P, NT, E])
        n_ps = m.psum("n", [P, NT, E])

        wo_loaded = m.sem("wo_loaded")
        w_loaded = m.sem("w_loaded")
        consts = m.sem("consts")
        tables_set = m.sem("tables_set")
        o_loaded = [m.sem(f"o_loaded{i}") for i in range(2)]
        x_loaded = m.sem("x_loaded")
        wo_hi_ready = m.sem("wo_hi_ready")
        wo_lo_ready = m.sem("wo_lo_ready")
        w_hi_ready = m.sem("w_hi_ready")
        w_lo_ready = m.sem("w_lo_ready")
        o_hi_ready = m.sem("o_hi_ready")
        o_lo_ready = [m.sem(f"o_lo_ready{i}") for i in range(2)]
        xT_lo_ready = m.sem("xT_lo_ready")
        y_ready = m.sem("y_ready")
        x1_ready = m.sem("x1_ready")
        norm_step = m.sem("norm_step")
        scan_step = m.sem("scan_step")
        route_step = m.sem("route_step")
        place_step = m.sem("place_step")
        var_ready = m.sem("var_ready")
        rstd_ready = m.sem("rstd_ready")
        xn_ready = m.sem("xn_ready")
        turned = m.sem("turned")
        xT_ready = m.sem("xT_ready")
        in_ready = m.sem("in_ready")
        act_in = m.sem("act_in")
        read_by_dve = m.sem("read_by_dve")
        gated = m.sem("gated")
        z_ready = m.sem("z_ready")
        sz_ready = m.sem("sz_ready")
        mixed = m.sem("mixed")
        out_ready = m.sem("out_ready")
        x2_ready = m.sem("x2_ready")
        x2_stored = m.sem("x2_stored")
        xn_stored = m.sem("xn_stored")
        logits = m.sem("logits")
        top_ready = m.sem("top_ready")
        exp_ready = m.sem("exp_ready")
        chosen_ready = m.sem("chosen_ready")
        counted = m.sem("counted")
        pair_ready = m.sem("pair_ready")
        scattered = m.sem("scattered")
        passed = m.sem("passed")
        block = ctx.enter_context(nc.Block())

        W_F, W_I, W_V, W_GATE, W_UP, W_Q = range(N_IN)
        FILLS = ([(w, c) for c in range(C) for w in (W_F, W_I, W_V)]
                 + [(w, c) for c in range(C) for w in (W_GATE, W_UP)] + [(W_Q, c) for c in range(C)])
        NF = len(FILLS)
        BY_ACT = [n for n, (w, _) in enumerate(FILLS) if w in (W_F, W_I, W_V, W_GATE)]
        BY_DVE = [n for n, (w, _) in enumerate(FILLS) if w in (W_V, W_GATE, W_UP)]

        def groups(eng, body):
            body(0, NG > 1)
            if NG > 2:
                with eng.Fori(1, NG - 1) as g:
                    body(g, True)
            if NG > 1:
                body(NG - 1, False)

        @block.sync
        def _(sp):
            def load_x(g):
                wait_from(sp, x1_ready, g * NT)
                waits_here(sp, passed)
                sp.dma_start(x[:], d["x"][bass.ds(g * GB, GB)].rearrange("b s d -> (b s) d").rearrange(
                    "(n p) d -> p n d", p=P)).then_inc(x_loaded, 16)

            def load_output(g, t):
                before_t = (t - 2) % NT
                wait_from(sp, o_lo_ready[before_t // HT], g * HT + (before_t % HT + 1 - (HT if t < 2 else 0)))
                waits_here(sp, passed)
                for b in range(BT):
                    sp.dma_start(oT[:, t % 2, :, b], d["oT"][bass.ds(g * GB + t * BT + b, 1)].rearrange(
                        "a p h s -> (a p) h s")).then_inc(o_loaded[t % 2], 16)

            def body(g, more):
                if more:
                    load_x(g + 1)
                    for t in range(NT):
                        load_output(g + 1, t)
                sp.wait_ge(x2_ready, g * NT + NT)
                waits_here(sp, passed)
                sp.dma_start(d["sum0"][bass.ds(g * GT, GT)].rearrange("(n p) d -> p n d", p=P), x2[:]
                             ).then_inc(x2_stored, 16)
                sp.wait_ge(xn_ready, g * (2 * NT) + 2 * NT)
                waits_here(sp, passed)
                sp.dma_start(d["tokens"][bass.ds(g * GT, GT)].rearrange("(n p) d -> p n d", p=P), xn[:]
                             ).then_inc(xn_stored, 16)

            sp.dma_start(wo, d["Wo"].rearrange("(h p) n -> p h n", p=P)).then_inc(wo_loaded, 16)
            load_x(0)
            for t in range(2):
                load_output(0, t)
            for n, name in ((W_F, "w_f"), (W_I, "w_i"), (W_V, "w_v"), (W_Q, "w_q"), (W_UP, "w_up"), (W_GATE, "w_gate")):
                sp.dma_start(w_in[:, n], d[name].rearrange("(c p) n -> p c n", p=P)).then_inc(w_loaded, 16)
            sp.dma_start(w_ro[:], d["w_ro"].rearrange("(c p) n -> p c n", p=P)).then_inc(w_loaded, 16)
            sp.dma_start(w_down[:], d["w_down"].rearrange("(c p) n -> p c n", p=P)).then_inc(w_loaded, 16)
            with nc.allow_non_contiguous_dma("256 numbers"):
                sp.dma_start(init[:], d["init_state"].rearrange("(c p) -> p c", p=P)).then_inc(w_loaded, 16)
            sp.dma_start(router[:], d["routerT"].rearrange("(c p) e -> p c e", p=P)).then_inc(w_loaded, 16)
            for t in range(2, NT):
                load_output(0, t)
            sp.wait_ge(consts, 9)
            sp.dma_start(d["tokens"][T:T + P, :], zero[:, 0:D]).then_inc(tables_set, 16)
            sp.dma_start(d["slots"].rearrange("(p e) w -> p e w", e=E), empty[:CAP]).then_inc(tables_set, 16)
            sp.dma_start(d["sum0"][T:T + P, :], zero[:, 0:D]).then_inc(tables_set, 16)
            sp.dma_start(d["sum1"][T:T + P, :], zero[:, 0:D]).then_inc(tables_set, 16)
            for g in range(NG):
                sp.dma_start(d["sum1"][g * GT:(g + 1) * GT, :].rearrange("(p r) d -> p (r d)", p=P), zero[:]
                             ).then_inc(tables_set, 16)
            sp.wait_ge(tables_set, 16 * (4 + NG))
            groups(sp, body)
            sp.wait_ge(x2_stored, 16 * NG)
            sp.wait_ge(xn_stored, 16 * NG)

        @block.gpsimd
        def _(pool):
            pool.memset(ident[:], 0.0).then_inc(consts, 1)
            pool.memset(before[:], 1.0).then_inc(consts, 1)
            pool.memset(ones[:], 1.0).then_inc(consts, 1)
            pool.memset(neg_half[:], -0.5).then_inc(consts, 1)
            pool.memset(zero[:], 0.0).then_inc(consts, 1)
            pool.memset(empty[:], 0.0).then_inc(consts, 1)
            pool.wait_ge(consts, 6)
            pool.affine_select(out=ident[:], in_=ident[:], compare_op=ALU.not_equal, fill=1.0, base=0,
                               pattern=[[-1, P]], channel_multiplier=1).then_inc(consts, 1)
            pool.affine_select(out=before[:], in_=before[:], compare_op=ALU.is_gt, fill=0.0, base=0,
                               pattern=[[1, P]], channel_multiplier=-1).then_inc(consts, 1)
            pool.iota(empty[:, :, 1], [[0, E]], base=T, channel_multiplier=1,
                      allow_small_or_imprecise_dtypes=True).then_inc(consts, 1)
            pool.iota(slot_base[:], [[-1, E]], base=SLOTS, channel_multiplier=0,
                      allow_small_or_imprecise_dtypes=True).then_inc(consts, 1)
            pool.iota(token[:], [[P, NT]], base=0, channel_multiplier=1,
                      allow_small_or_imprecise_dtypes=True).then_inc(consts, 1)

            def deviation(g, k):
                pool.wait_ge(var_ready, g * 2 + (k + 1))
                pool.tensor_tensor(rstd[:], var[:], neg_half[:], ALU.pow).then_inc(rstd_ready, 1)

            def split_output(g, t):
                pool.wait_ge(o_hi_ready, g * NT + (t + 1))
                wait_from(pool, y_ready, g * NT + (t - 1))
                pool.tensor_tensor(oT_lo[:, t % 2], oT[:, t % 2].rearrange("p h b s -> p h (b s)"), oT_hi[:, t % 2],
                                   ALU.subtract).then_inc(o_lo_ready[0], 1)

            def send(g, tiles):
                for t in tiles:
                    pool.wait_ge(pair_ready, g * NT + (t + 1))
                    waits_here(pool, passed)
                    for k in range(TOP):
                        pool.indirect_dma_start(
                            out=d["slots"], out_offset=bass.IndirectOffsetOnAxis(ap=place[:, t, k:k + 1], axis=0),
                            in_=pair[:, t, k], in_offset=None, bounds_check=SLOTS - 1, oob_is_err=False
                        ).then_inc(scattered, 16)

            def body(g, more):
                if more:
                    for t in range(HT):
                        split_output(g + 1, t)
                if not isinstance(g, int) or g > 0:
                    send(g - 1, range(HT))
                deviation(g, 1)
                if not isinstance(g, int) or g > 0:
                    send(g - 1, range(HT, NT - 1))
                if more:
                    deviation(g + 1, 0)
                if not isinstance(g, int) or g > 0:
                    send(g - 1, range(NT - 1, NT))

            for t in range(HT):
                split_output(0, t)
            deviation(0, 0)
            pool.wait_ge(tables_set, 16 * (4 + NG))
            groups(pool, body)
            send(NG - 1, range(NT))
            pool.wait_ge(scattered, 16 * NG * NT * TOP)

        @block.scalar
        def _(act):
            def split_output(g, t):
                act.wait_ge(o_loaded[t % 2], g * (NT // 2 * BT * 16) + BT * 16 * (t // 2 + 1))
                wait_from(act, y_ready, g * NT + (t - 1))
                act.activation(oT_hi[:, t % 2], oT[:, t % 2].rearrange("p h b s -> p h (b s)"), ACT.Copy
                               ).then_inc(o_hi_ready, 1)

            def body(g, more):
                for c in range(C):
                    act.wait_ge(turned, g * (2 * C) + (c + 1))
                    wait_from(act, in_ready, g * NF)
                    act.activation(xT_hi[:, c], turn_ps[c][:], ACT.Copy).then_inc(xT_ready, 1)
                for n in BY_ACT:
                    if more and n in (BY_ACT[0], BY_ACT[3]):
                        split_output(g + 1, BY_ACT.index(n) // 3)
                    w, c = FILLS[n]
                    act.wait_ge(in_ready, g * NF + (n + 1))
                    out = {W_F: f, W_I: g_, W_V: sv, W_GATE: sv}[w]
                    if w == W_GATE:
                        act.wait_ge(gated, g * C + (c + 1))
                    act.activation(out[:, c], in_ps[n % 3][:], ACT.Tanh if w == W_F else ACT.Sigmoid
                                   ).then_inc(act_in, 1)
                for c in range(C):
                    act.wait_ge(z_ready, g * C + (c + 1))
                    act.activation(sz[:, c], z[:, c], ACT.Sigmoid).then_inc(sz_ready, 1)
                if more:
                    split_output(g + 1, 2)
                    split_output(g + 1, 3)
                for c in range(C):
                    act.wait_ge(turned, g * (2 * C) + (C + c + 1))
                    act.activation(xT[:, c], turn_ps[c][:], ACT.Copy).then_inc(xT_ready, 1)
                for t in range(NT):
                    act.wait_ge(top_ready, g + 1)
                    act.activation(expd[:, t], l_ps[:, t], ACT.Exp, bias=top_logit[:, t:t + 1],
                                   accum_out=esum[:, t:t + 1]).then_inc(exp_ready, 1)

            act.wait_ge(wo_loaded, 16)
            act.activation(wo_hi[:], wo, ACT.Copy).then_inc(wo_hi_ready, 1)
            for t in range(2):
                split_output(0, t)
            act.wait_ge(w_loaded, 16 * 10)
            act.activation(w_in_hi[:], w_in, ACT.Copy).then_inc(w_hi_ready, 1)
            for t in range(2, NT):
                split_output(0, t)
            act.wait_ge(w_lo_ready, 1)
            groups(act, body)

        @block.vector
        def _(dve):
            def add_output(g, t):
                dve.wait_ge(x_loaded, g * 16 + 16)
                dve.wait_ge(y_ready, g * NT + (t + 1))
                dve.tensor_tensor(x1[:, t], y_ps[t % 2][:, 0:D], x[:, t], ALU.add).then_inc(x1_ready, 1)

            def split_output(g, t):
                dve.wait_ge(o_hi_ready, g * NT + (t + 1))
                wait_from(dve, y_ready, g * NT + (t - 1))
                dve.tensor_tensor(oT_lo[:, t % 2], oT[:, t % 2].rearrange("p h b s -> p h (b s)"), oT_hi[:, t % 2],
                                  ALU.subtract).then_inc(o_lo_ready[1], 1)

            def linked(step, base):
                counts = itertools.count(1)

                def link(*instructions):
                    for ins in instructions:
                        count = next(counts)
                        ins.then_inc(step, 1)
                    dve.wait_ge(step, base + count)
                    waits_here(dve, passed)
                return link

            def norm(g, k):
                src, ready = ((x1, x1_ready), (x2, x2_ready))[k]
                dve.wait_ge(ready, g * NT + NT)
                link = linked(norm_step, g * (4 * NT) + k * (2 * NT))
                link(*[dve.bn_stats(stats[:, t], src[:, t]) for t in range(NT)])
                link(*[dve.bn_aggr(mv[:, t], stats[:, t]) for t in range(NT)])
                dve.tensor_scalar(var[:], mv[:, :, 1], LN_EPS, None, ALU.add).then_inc(var_ready, 1)
                dve.wait_ge(rstd_ready, g * 2 + (k + 1))
                if k == 0:
                    wait_from(dve, xn_stored, g * 16)
                    wait_from(dve, turned, g * (2 * C))
                else:
                    dve.wait_ge(turned, g * (2 * C) + C)
                for t in range(NT):
                    dve.tensor_scalar(xn[:, t], src[:, t], mv[:, t, 0:1], rstd[:, t:t + 1],
                                      ALU.subtract, ALU.mult).then_inc(xn_ready, 1)

            def encode_places(g):
                link = linked(place_step, g * PLACE_STEPS)
                dve.wait_ge(counted, g + 1)
                link(dve.scalar_tensor_tensor(out=tmp[:], in0=n_ps[:], scalar=float(-E),
                                              in1=slot_base[:].unsqueeze(1).broadcast_to([P, NT, E]),
                                              op0=ALU.mult, op1=ALU.add),
                     dve.scalar_tensor_tensor(out=kept[:], in0=n_ps[:], scalar=float(CAP), in1=chosen[:],
                                              op0=ALU.is_lt, op1=ALU.mult))
                link(dve.tensor_tensor(code[:], tmp[:], kept[:], ALU.mult))
                link(*[dve.max(code8[:, t], code[:, t]) for t in range(NT)])

            def find_weights(g):
                link = linked(place_step, g * PLACE_STEPS + 3 + NT)
                wait_from(dve, scattered, g * (16 * NT * TOP))
                link(dve.tensor_scalar(place[:], code8[:], -1.0, float(SLOTS), ALU.mult, ALU.add),
                     dve.tensor_copy(pair[:, :, :, 1], token[:].unsqueeze(2).broadcast_to([P, NT, TOP])),
                     *[dve.tensor_tensor(same[:, t], code8[:, t].unsqueeze(2).broadcast_to([P, TOP, E]),
                                         code[:, t].unsqueeze(1).broadcast_to([P, TOP, E]), ALU.is_equal)
                       for t in range(NT)])

            def pair_weights(g):
                link = linked(place_step, g * PLACE_STEPS + 5 + 2 * NT)
                link(*[dve.tensor_tensor(same[:, t], same[:, t],
                                         probs[:, t].unsqueeze(1).broadcast_to([P, TOP, E]), ALU.mult)
                       for t in range(NT)])
                for t in range(NT):
                    dve.tensor_reduce(pair[:, t, :, 0], same[:, t], AX_X, ALU.add).then_inc(pair_ready, 1)
                for t in range(NT):
                    link(dve.tensor_tensor(taken[:], taken[:], chosen[:, t], ALU.add))
                link(dve.tensor_scalar(token[:], token[:], float(GT), None, ALU.add))

            def body(g, more):
                for c in range(C):
                    dve.wait_ge(xT_ready, g * (2 * C) + (c + 1))
                    wait_from(dve, in_ready, g * NF)
                    dve.tensor_tensor(xT_lo[:, c], turn_ps[c][:], xT_hi[:, c], ALU.subtract).then_inc(xT_lo_ready, 1)
                later = not isinstance(g, int) or g > 0
                if later:
                    encode_places(g - 1)
                link = linked(scan_step, g * (3 * C))
                for c in range(C):
                    n = c * 3 + 2
                    dve.wait_ge(act_in, g * len(BY_ACT) + (n + 1))
                    dve.tensor_tensor(sv[:, c], in_ps[n % 3][:], sv[:, c], ALU.mult).then_inc(read_by_dve, 1)
                    dve.wait_ge(read_by_dve, g * len(BY_DVE) + (c + 1))
                    dve.tensor_tensor(g_[:, c], g_[:, c], sv[:, c], ALU.mult).then_inc(gated, 1)
                    dve.wait_ge(gated, g * C + (c + 1))
                    fs = f[:, c].rearrange("p (b s) -> p b s", s=S)[:, :, 0]
                    gs = g_[:, c].rearrange("p (b s) -> p b s", s=S)[:, :, 0]
                    link(dve.scalar_tensor_tensor(out=gs, in0=fs, scalar=init[:, c:c + 1], in1=gs,
                                                  op0=ALU.mult, op1=ALU.add))
                    link(dve.memset(fs, 0.0))
                    link(dve.tensor_tensor_scan(states[:, c], f[:, c], g_[:, c], 0.0, ALU.mult, ALU.add))
                    if later and c == 0:
                        find_weights(g - 1)
                for c in range(C):
                    n = 3 * C + 2 * c
                    dve.wait_ge(act_in, g * len(BY_ACT) + (3 * C + c + 1))
                    dve.tensor_tensor(sv[:, c], in_ps[n % 3][:], sv[:, c], ALU.mult).then_inc(read_by_dve, 1)
                    dve.wait_ge(read_by_dve, g * len(BY_DVE) + (C + 2 * c + 1))
                    dve.wait_ge(in_ready, g * NF + (n + 2))
                    dve.tensor_tensor(mlp[:, c], in_ps[(n + 1) % 3][:], sv[:, c], ALU.mult
                                      ).then_inc(read_by_dve, 1)
                for c in range(C):
                    n = 5 * C + c
                    dve.wait_ge(in_ready, g * NF + (n + 1))
                    dve.tensor_tensor(z[:, c], in_ps[n % 3][:], states[:, c], ALU.mult).then_inc(z_ready, 1)
                for c in range(C):
                    dve.wait_ge(sz_ready, g * C + (c + 1))
                    dve.tensor_tensor(sz[:, c], z[:, c], sz[:, c], ALU.mult).then_inc(mixed, 1)
                if later:
                    pair_weights(g - 1)
                if more:
                    split_output(g + 1, 2)
                wait_from(dve, x2_stored, g * 16)
                for t in range(NT):
                    dve.wait_ge(out_ready, g * NT + (t + 1))
                    dve.tensor_tensor(x2[:, t], in_ps[t % 3][:, 0:D], x1[:, t], ALU.add).then_inc(x2_ready, 1)
                if more:
                    dve.wait_ge(x2_ready, g * NT + NT)
                    add_output(g + 1, 0)
                    add_output(g + 1, 1)
                norm(g, 1)
                if more:
                    split_output(g + 1, 3)
                    add_output(g + 1, 2)
                link = linked(route_step, g * (3 + 2 * NT))
                dve.wait_ge(logits, g * NT + NT)
                link(dve.tensor_reduce(top_logit[:], l_ps[:], AX_X, ALU.max))
                dve.tensor_scalar(top_logit[:], top_logit[:], -1.0, None, ALU.mult).then_inc(top_ready, 1)
                dve.wait_ge(exp_ready, g * NT + NT)
                link(dve.reciprocal(resum[:], esum[:]))
                link(dve.tensor_tensor(probs[:], expd[:], resum[:].unsqueeze(2).broadcast_to([P, NT, E]), ALU.mult))
                link(*[dve.max(top8[:, t], probs[:, t]) for t in range(NT)])
                link(*[dve.match_replace(rest[:, t], top8[:, t], probs[:, t], -1.0) for t in range(NT)])
                dve.tensor_scalar(chosen[:], rest[:], 0.0, None, ALU.is_lt).then_inc(chosen_ready, 1)
                if more:
                    add_output(g + 1, 3)
                    norm(g + 1, 0)

            PLACE_STEPS = 4 * NT + 6
            dve.wait_ge(consts, 11)
            dve.memset(taken[:], 0.0).then_inc(consts, 1)
            dve.wait_ge(consts, 12)
            dve.wait_ge(wo_hi_ready, 1)
            dve.tensor_tensor(wo_lo[:], wo, wo_hi[:], ALU.subtract).then_inc(wo_lo_ready, 1)
            dve.wait_ge(w_hi_ready, 1)
            dve.tensor_tensor(w_in_lo[:], w_in, w_in_hi[:], ALU.subtract).then_inc(w_lo_ready, 1)
            for t in range(NT):
                if t >= 2:
                    split_output(0, t)
                add_output(0, t)
            norm(0, 0)
            dve.wait_ge(w_lo_ready, 1)
            groups(dve, body)
            encode_places(NG - 1)
            find_weights(NG - 1)
            pair_weights(NG - 1)

        @block.tensor
        def _(pe):
            pe.wait_ge(wo_lo_ready, 1)
            pe.wait_ge(consts, 12)

            def turn(g, k):
                pe.wait_ge(xn_ready, g * (2 * NT) + (k + 1) * NT)
                for c in range(C):
                    for t in range(NT):
                        last = pe.transpose(turn_ps[c][:, t * P:(t + 1) * P], xn[:, t, c * P:(c + 1) * P], ident[:])
                    last.then_inc(turned, 1)
                pe.wait_ge(xT_ready, g * (2 * C) + (k + 1) * C)
                pe.wait_ge(xT_lo_ready, g * C + C)

            def project_output(g, t):
                pe.wait_ge(o_lo_ready[t // HT], g * HT + (t % HT + 1))
                wait_from(pe, x1_ready, g * NT + (t - 1))
                n = 0
                for o, w in ((oT_hi, wo_hi), (oT_hi, wo_lo), (oT_lo, wo_hi)):
                    for h in range(NH):
                        last = pe.matmul(y_ps[t % 2][:, 0:D], o[:, t % 2, h], w[:, h], start=n == 0,
                                         stop=n == 3 * NH - 1)
                        n += 1
                last.then_inc(y_ready, 1)

            def body(g, more):
                turn(g, 0)
                for n, (w, c) in enumerate(FILLS):
                    p = n - 3
                    if p >= 0:
                        if p in BY_DVE:
                            pe.wait_ge(read_by_dve, g * len(BY_DVE) + (BY_DVE.index(p) + 1))
                        else:
                            pe.wait_ge(act_in, g * len(BY_ACT) + (BY_ACT.index(p) + 1))
                    else:
                        wait_from(pe, x2_ready, g * NT)
                    i = 0
                    for u, v in ((w_in_hi, xT_hi), (w_in_hi, xT_lo), (w_in_lo, xT_hi)):
                        for r in range(C):
                            last = pe.matmul(in_ps[n % 3][:], u[:, w, r, c * P:(c + 1) * P], v[:, r], start=i == 0,
                                             stop=i == 3 * C - 1)
                            i += 1
                    last.then_inc(in_ready, 1)
                if more:
                    project_output(g + 1, 0)
                    project_output(g + 1, 1)
                pe.wait_ge(mixed, g * C + C)
                for t in range(NT):
                    if t >= 3:
                        pe.wait_ge(x2_ready, g * NT + (t - 2))
                    n = 0
                    for a, w in ((sz, w_ro), (mlp, w_down)):
                        for c in range(C):
                            last = pe.matmul(in_ps[t % 3][:, 0:D], a[:, c, t * P:(t + 1) * P], w[:, c], start=n == 0,
                                             stop=n == 2 * C - 1)
                            n += 1
                    last.then_inc(out_ready, 1)
                if more:
                    project_output(g + 1, 2)
                turn(g, 1)
                wait_from(pe, exp_ready, g * NT)
                for t in range(NT):
                    for c in range(C):
                        last = pe.matmul(l_ps[:, t], xT[:, c, t * P:(t + 1) * P], router[:, c], start=c == 0,
                                         stop=c == C - 1)
                    last.then_inc(logits, 1)
                if more:
                    project_output(g + 1, 3)
                pe.wait_ge(chosen_ready, g + 1)
                pe.matmul(n_ps[:], ones[:], taken[:].unsqueeze(1).broadcast_to([P, NT, E]), start=True, stop=False,
                          skip_group_check=True)
                for t in range(NT - 1):
                    pe.matmul(n_ps[:, t + 1:], ones[:], chosen[:, t:t + 1].broadcast_to([P, NT - 1 - t, E]),
                              start=False, stop=False, skip_group_check=True)
                pe.matmul(n_ps[:], before[:], chosen[:], start=False, stop=True, skip_group_check=True
                          ).then_inc(counted, 1)

            for t in range(NT):
                project_output(0, t)
            pe.wait_ge(w_loaded, 16 * 10)
            pe.wait_ge(w_lo_ready, 1)
            groups(pe, body)


def expert_stage(nc, d):
    B, S, D = d["x"].shape
    T = B * S
    C = D // P
    E = d["experts"]
    NT = T // P
    F = d["w_gate"].shape[2]
    U = 8
    AHEAD = 5
    PIECES = 4
    assert F == P and E % U == 0 and E // U >= 2 and NT % PIECES == 0

    with ExitStack() as ctx:
        m = Memory(nc, ctx, "moe")
        pairs = m.sbuf("pairs", [P, E, 2])
        ids = m.sbuf("ids", [P, E], mybir.dt.int32)
        weight = m.sbuf("weight", [P, E])
        rows = m.sbuf("rows", [P, U], mybir.dt.int32)
        ident = m.sbuf("ident", [P, P])
        wg = m.sbuf("wg", [P, U, C, F])
        wu = m.sbuf("wu", [P, U, C, F])
        wd = m.sbuf("wd", [P, U, D])
        xg = m.sbuf("xg", [P, U, D])
        xT = m.sbuf("xT", [P, 2, C, P])
        sig = m.sbuf("sig", [P, 2, P])
        gate = m.sbuf("gate", [P, 2, P])
        hid = m.sbuf("hid", [P, 2, P])
        yw = m.sbuf("yw", [P, U, D])
        sums = m.sbuf("sums", [P, 2, NT, D])
        total = m.sbuf("total", [P, NT, D])
        t_ps = [m.psum(f"t{i}", [P, C, P]) for i in range(2)]
        gu_ps = [m.psum(f"gu{i}", [P, 2, P]) for i in range(2)]
        y_ps = [m.psum(f"y{i}", [P, D]) for i in range(2)]

        consts = m.sem("consts")
        pairs_loaded = m.sem("pairs_loaded")
        ids_ready = m.sem("ids_ready")
        rows_ready = m.sem("rows_ready")
        w_loaded = [m.sem(f"w_loaded{i}") for i in range(U // 2)]
        gathered = [m.sem(f"gathered{i}") for i in range(U)]
        turned = m.sem("turned")
        xT_ready = m.sem("xT_ready")
        gu_ready = m.sem("gu_ready")
        sig_ready = m.sem("sig_ready")
        gate_ready = m.sem("gate_ready")
        hid_ready = m.sem("hid_ready")
        y_ready = m.sem("y_ready")
        yw_ready = m.sem("yw_ready")
        added = [m.sem(f"added{i}") for i in range(2)]
        sums_loaded = [m.sem(f"sums_loaded{i}") for i in range(PIECES)]
        total_ready = m.sem("total_ready")
        stored = m.sem("stored")
        passed = m.sem("passed")
        block = ctx.enter_context(nc.Block())

        NP = NT // PIECES

        def experts(eng, body):
            body(0, False)
            if E > 2 * U:
                with eng.Fori(1, E // U - 1) as i:
                    body(i, False)
            body(E // U - 1, True)

        @block.sync
        def _(sp):
            sp.dma_start(pairs[:], d["slots"].rearrange("(p e) w -> p e w", e=E)).then_inc(pairs_loaded, 16)

            def body(i, last):
                for k in range(0, U, 2):
                    wait_from(sp, y_ready, i * U + (k - U + 2))
                    waits_here(sp, passed)
                    for buf, name in ((wg, "w_gate"), (wu, "w_up")):
                        sp.dma_start(buf[:, k:k + 2].rearrange("p e c f -> p (e c) f"),
                                     d[name][bass.ds(i * U + k, 2)].rearrange(
                                         "a (c p) f -> p (a c) f", p=P)).then_inc(w_loaded[k // 2], 16)
                    sp.dma_start(wd[:, k:k + 2], d["w_down"][bass.ds(i * U + k, 2)].rearrange(
                        "a p n -> p a n")).then_inc(w_loaded[k // 2], 16)

            experts(sp, body)
            for n in range(2):
                sp.wait_ge(added[n], 16 * (E // 2))
            for c in range(PIECES):
                for n in range(2):
                    sp.dma_start(sums[:, n, c * NP:(c + 1) * NP], d[f"sum{n}"][c * NP * P:(c + 1) * NP * P].rearrange(
                        "(n p) d -> p n d", p=P)).then_inc(sums_loaded[c], 16)
            for c in range(PIECES):
                sp.wait_ge(total_ready, c + 1)
                sp.dma_start(d["out"].rearrange("b s d -> (b s) d")[c * NP * P:(c + 1) * NP * P].rearrange(
                    "(n p) d -> p n d", p=P), total[:, c * NP:(c + 1) * NP]).then_inc(stored, 16)
            sp.wait_ge(stored, 16 * PIECES)

        @block.gpsimd
        def _(pool):
            pool.memset(ident[:], 0.0).then_inc(consts, 1)
            pool.wait_ge(consts, 1)
            pool.affine_select(out=ident[:], in_=ident[:], compare_op=ALU.not_equal, fill=1.0, base=0,
                               pattern=[[-1, P]], channel_multiplier=1).then_inc(consts, 1)
            pool.wait_ge(ids_ready, 1)
            last_row = pool.to_reg(T + P - 1)

            def gather(i, k):
                wait_from(pool, turned, i * U + (k - U + 1))
                pool.wait_ge(rows_ready, i * U + (k + 1))
                waits_here(pool, passed)
                pool.indirect_dma_start(out=xg[:, k], out_offset=None, in_=d["tokens"],
                                        in_offset=bass.IndirectOffsetOnAxis(ap=rows[:, k:k + 1], axis=0),
                                        bounds_check=last_row, oob_is_err=True).then_inc(gathered[k], 16)

            for k in range(AHEAD):
                gather(0, k)

            def body(i, last):
                for k in range(U):
                    if not (last and k + AHEAD >= U):
                        gather(i + (k + AHEAD) // U, (k + AHEAD) % U)
                    pool.wait_ge(yw_ready, i * U + (k + 1))
                    wait_from(pool, added[k % 2], i * (U // 2 * 16) + k // 2 * 16)
                    waits_here(pool, passed)
                    pool.indirect_dma_start(out=d[f"sum{k % 2}"],
                                            out_offset=bass.IndirectOffsetOnAxis(ap=rows[:, k:k + 1], axis=0),
                                            in_=yw[:, k], in_offset=None, bounds_check=last_row,
                                            oob_is_err=True, compute_op=ALU.add).then_inc(added[k % 2], 16)

            experts(pool, body)

        @block.scalar
        def _(act):
            def columns(i, k):
                act.wait_ge(turned, i * U + (k + 1))
                wait_from(act, gu_ready, i * U + (k - 1))
                act.activation(xT[:, k % 2], t_ps[k % 2][:], ACT.Copy).then_inc(xT_ready, 1)

            def sigmoid(i, k):
                act.wait_ge(gu_ready, i * U + (k + 1))
                act.activation(sig[:, k % 2], gu_ps[k % 2][:, 0], ACT.Sigmoid).then_inc(sig_ready, 1)

            def body(i, last):
                for k in range(U):
                    if not (last and k + 2 >= U):
                        columns(i + (k + 2) // U, (k + 2) % U)
                    if not (last and k + 1 >= U):
                        sigmoid(i + (k + 1) // U, (k + 1) % U)
                    act.wait_ge(y_ready, i * U + (k + 1))
                    wait_from(act, added[k % 2], i * (U // 2 * 16) + (k // 2 - U // 2 + 1) * 16)
                    act.activation(yw[:, k], y_ps[k % 2][:], ACT.Copy, scale=weight[:, bass.ds(i * U + k, 1)]
                                   ).then_inc(yw_ready, 1)

            columns(0, 0)
            columns(0, 1)
            sigmoid(0, 0)
            act.wait_ge(ids_ready, 2)
            experts(act, body)

        @block.vector
        def _(dve):
            dve.wait_ge(pairs_loaded, 16)
            dve.tensor_copy(ids[:], pairs[:, :, 1]).then_inc(ids_ready, 1)
            dve.tensor_copy(weight[:], pairs[:, :, 0]).then_inc(ids_ready, 1)
            dve.wait_ge(ids_ready, 2)

            def take_rows(i, k):
                wait_from(dve, added[k % 2], i * (U // 2 * 16) + (k // 2 - U // 2 + 1) * 16)
                dve.tensor_copy(rows[:, k:k + 1], ids[:, bass.ds(i * U + k, 1)]).then_inc(rows_ready, 1)

            for k in range(AHEAD):
                take_rows(0, k)

            def body(i, last):
                for k in range(U):
                    if not (last and k + AHEAD >= U):
                        take_rows(i + (k + AHEAD) // U, (k + AHEAD) % U)
                    dve.wait_ge(sig_ready, i * U + (k + 1))
                    dve.tensor_tensor(gate[:, k % 2], gu_ps[k % 2][:, 0], sig[:, k % 2], ALU.mult
                                      ).then_inc(gate_ready, 1)
                    dve.wait_ge(gate_ready, i * U + (k + 1))
                    dve.tensor_tensor(hid[:, k % 2], gu_ps[k % 2][:, 1], gate[:, k % 2], ALU.mult
                                      ).then_inc(hid_ready, 1)

            experts(dve, body)
            for c in range(PIECES):
                dve.wait_ge(sums_loaded[c], 32)
                sl = slice(c * NP, (c + 1) * NP)
                dve.tensor_tensor(total[:, sl], sums[:, 0, sl], sums[:, 1, sl], ALU.add).then_inc(total_ready, 1)

        @block.tensor
        def _(pe):
            pe.wait_ge(consts, 2)

            def turn(i, k):
                pe.wait_ge(gathered[k], i * 16 + 16)
                wait_from(pe, xT_ready, i * U + (k - 1))
                for c in range(C):
                    last = pe.transpose(t_ps[k % 2][:, c], xg[:, k, c * P:(c + 1) * P], ident[:])
                last.then_inc(turned, 1)

            def gate_up(i, k):
                pe.wait_ge(w_loaded[k // 2], i * 48 + 48)
                pe.wait_ge(xT_ready, i * U + (k + 1))
                wait_from(pe, hid_ready, i * U + (k - 1))
                for n, w in enumerate((wg, wu)):
                    for c in range(C):
                        last = pe.matmul(gu_ps[k % 2][:, n], w[:, k, c], xT[:, k % 2, c], start=c == 0,
                                         stop=c == C - 1)
                last.then_inc(gu_ready, 1)

            def down(i, k):
                pe.wait_ge(hid_ready, i * U + (k + 1))
                wait_from(pe, yw_ready, i * U + (k - 1))
                pe.matmul(y_ps[k % 2][:], hid[:, k % 2], wd[:, k], start=True, stop=True).then_inc(y_ready, 1)

            turn(0, 0)
            turn(0, 1)
            gate_up(0, 0)

            def body(i, last):
                for k in range(U):
                    if not (last and k + 2 >= U):
                        turn(i + (k + 2) // U, (k + 2) % U)
                    if not (last and k + 1 >= U):
                        gate_up(i + (k + 1) // U, (k + 1) % U)
                    down(i, k)

            experts(pe, body)


def perceiver_layer(nc, d):
    B, S, D = d["x"].shape
    T = B * S
    experts, top, capacity = d["routerT"].shape[1], 8, P
    NH = d["Wq"].shape[1] // P
    KH = d["Wk"].shape[1] // P

    def scratch(name, shape):
        return nc.dram_tensor(f"scratch_{name}", shape, F32).ap()

    d = dict(d, experts=experts, top=top, capacity=capacity,
             qT=scratch("qT", (B, P, NH, S)), rq=scratch("rq", (P, B * NH * S // P)),
             rden=scratch("rden", (B * KH, NH // KH * S // P, P)), oT=scratch("oT", (B, P, NH, S)),
             tokens=scratch("tokens", (T + P, D)), slots=scratch("slots", (experts * capacity, 2)),
             sum0=scratch("sum0", (T + P, D)), sum1=scratch("sum1", (T + P, D)))
    query_stage(nc, d)
    attention_stage(nc, d)
    recurrent_stage(nc, dict(d, w_up=d["rnn_w_up"], w_gate=d["rnn_w_gate"], w_down=d["rnn_w_down"]))
    expert_stage(nc, dict(d, w_up=d["moe_w_up"], w_gate=d["moe_w_gate"], w_down=d["moe_w_down"]))


def kernel(**inputs):
    import numpy as np
    import concourse.bacc as bacc
    from concourse.bass_utils import run_bass_kernel_spmd

    given = {name: np.ascontiguousarray(a) for name, a in inputs.items()}
    context = given["ctx_2048"]
    B, K, D = context.shape
    ctxT = np.zeros((B, D // 128, 128, K + K % 2), context.dtype)
    ctxT[..., :K] = context.transpose(0, 2, 1).reshape(B, D // 128, 128, K)
    arrays = {
        "x": given["x"], "ctxT": ctxT,
        "Wq": given["L0_xattn_Wq"], "Wk": given["L0_xattn_Wk"], "Wv": given["L0_xattn_Wv"],
        "Wo": given["L0_xattn_Wo"],
        "q_norm_w": given["L0_xattn_q_norm_w"], "k_norm_w": given["L0_xattn_k_norm_w"],
        "w_f": given["L0_attn_w_f"], "w_i": given["L0_attn_w_i"], "w_v": given["L0_attn_w_v"],
        "w_q": given["L0_attn_w_q"], "w_ro": given["L0_attn_w_ro"],
        "rnn_w_up": given["L0_attn_w_up"], "rnn_w_gate": given["L0_attn_w_gate"],
        "rnn_w_down": given["L0_attn_w_down"], "init_state": given["L0_attn_init_state"],
        "routerT": np.ascontiguousarray(given["L0_ffn_gate_w"].T),
        "moe_w_gate": given["L0_ffn_w_gate"], "moe_w_up": given["L0_ffn_w_up"],
        "moe_w_down": given["L0_ffn_w_down"],
    }
    nc = bacc.Bacc("TRN2", target_bir_lowering=False, num_devices=1)
    d = {name: nc.dram_tensor(name, a.shape, mybir.dt.from_np(a.dtype), kind="ExternalInput").ap()
         for name, a in arrays.items()}
    d["keys"] = K
    d["out"] = nc.dram_tensor("out", given["x"].shape, F32, kind="ExternalOutput").ap()
    perceiver_layer(nc, d)
    r = run_bass_kernel_spmd(nc, [arrays], core_ids=[0])
    return r.results[0]["out"]
```
